# Optimizing a Trainium2 kernel written in Bass

```python
import numpy as np
import jax
import jax.numpy as jnp

def _softmax(x, axis=-1):
    return jax.nn.softmax(x, axis=axis)

def _gelu(x):
    return jax.nn.gelu(x, approximate=True)

def _silu(x):
    return jax.nn.silu(x)

def _sigmoid(x):
    return jax.nn.sigmoid(x)

def _layernorm(x, axis=-1, eps=1e-05):
    m = jnp.mean(x, axis=axis, keepdims=True)
    v = jnp.var(x, axis=axis, keepdims=True)
    return (x - m) / jnp.sqrt(v + eps)

def _scatter_add(tgt, idx, src, axis=0):
    return tgt.at[idx].add(src)

def _segment_sum(src, seg, n):
    return jax.ops.segment_sum(src, seg, n)
kernel_name = 'mk_xattn_seq_d2_seqx_r8_058e45'

def setup_inputs(seed: int=0):
    np.random.seed(seed)
    _w = jnp.asarray

    def _rec_inputs():
        import jax
        import jax.numpy as jnp
        _rk = jax.random.key(seed)
        x = -0.0002928 + 1 * jax.random.normal(jax.random.fold_in(_rk, 1), (8, 256, 128), jnp.float32)
        _lenS = 256 - jax.random.randint(jax.random.fold_in(_rk, 7), (8,), 0, max(1, 256 // 4) + 1, jnp.int32)
        _lenS2 = 512 - jax.random.randint(jax.random.fold_in(_rk, 8), (8,), 0, max(1, 512 // 4) + 1, jnp.int32)
        _ctx_1024P = jax.random.normal(jax.random.fold_in(_rk, 11), (8, 16, 128), jnp.float32)
        _ctx_1024c = jax.random.dirichlet(jax.random.fold_in(_rk, 511), 0.3 * jnp.ones((16,), jnp.float32), (8, 512))
        _ctx_1024t = jnp.einsum('bsk,bkd->bsd', _ctx_1024c, _ctx_1024P)
        _ctx_1024t = _ctx_1024t * jax.lax.rsqrt(jnp.mean(jnp.square(_ctx_1024t)) + 1e-12) * 0.953939
        ctx_1024 = -1.39393e-06 + 0.999914 * (_ctx_1024t + 0.3 * jax.random.normal(jax.random.fold_in(_rk, 611), (8, 512, 128), jnp.float32))
        _validS = jnp.arange(256)[None, :] < _lenS[:, None]
        _validS2 = jnp.arange(512)[None, :] < _lenS2[:, None]
        _causal = jnp.tril(jnp.ones((256, 256), dtype=bool))
        mask_BxS2_bf1 = jnp.ones((8, 512), dtype=bool)
        return (x, ctx_1024, mask_BxS2_bf1)
    x, ctx_1024, mask_BxS2_bf1 = _rec_inputs()

    def _L0_xattn_setup():
        import jax, jax.numpy as jnp
        import numpy as np
        B, L, M, D, H, FF, W = (2, 256, 256, 128, 16, 512, 64)
        DH = D // H

        def _layernorm(x, g, b, eps=1e-05):
            mu = x.mean(-1, keepdims=True)
            var = ((x - mu) ** 2).mean(-1, keepdims=True)
            return (x - mu) / jnp.sqrt(var + eps) * g + b

        def _mha(qx, kx, wq, bq, wk, bk, wv, bv, wo, bo, mask, bias):
            Bq, Lq, _ = qx.shape
            Lk = kx.shape[1]
            q = (qx @ wq + bq).reshape(Bq, Lq, H, DH).transpose(0, 2, 1, 3)
            k = (kx @ wk + bk).reshape(Bq, Lk, H, DH).transpose(0, 2, 1, 3)
            v = (kx @ wv + bv).reshape(Bq, Lk, H, DH).transpose(0, 2, 1, 3)
            s = jnp.einsum('bhqd,bhkd->bhqk', q, k) / jnp.sqrt(jnp.asarray(DH, qx.dtype))
            if bias is not None:
                s = s + bias[None]
            if mask is not None:
                s = jnp.where(mask[None, None], s, jnp.asarray(-1000000000.0, qx.dtype))
            a = jax.nn.softmax(s, axis=-1)
            o = jnp.einsum('bhqk,bhkd->bhqd', a, v).transpose(0, 2, 1, 3).reshape(Bq, Lq, D)
            return o @ wo + bo

        def _forward(x, mem, swq, sbq, swk, sbk, swv, sbv, swo, sbo, cwq, cbq, cwk, cbk, cwv, cbv, cwo, cbo, w1, b1, w2, b2, g1, be1, g2, be2, g3, be3):
            i = jnp.arange(L)[:, None]
            j = jnp.arange(L)[None, :]
            mask = (j <= i) & (i - j < W)
            slopes = 2.0 ** (-8.0 * jnp.arange(1, H + 1, dtype=x.dtype) / H)
            bias = slopes[:, None, None] * (j - i).astype(x.dtype)[None]
            sa = _mha(x, x, swq, sbq, swk, sbk, swv, sbv, swo, sbo, mask, bias)
            x = _layernorm(x + sa, g1, be1)
            ca = _mha(x, mem, cwq, cbq, cwk, cbk, cwv, cbv, cwo, cbo, None, None)
            x = _layernorm(x + ca, g2, be2)
            ff = jax.nn.gelu(x @ w1 + b1, approximate=False) @ w2 + b2
            return _layernorm(x + ff, g3, be3)
        key = jax.random.key(seed)
        ks = jax.random.split(key, 16)
        s = 0.02
        inp = {'x': jax.random.normal(ks[0], (B, L, D), jnp.float32), 'mem': jax.random.normal(ks[1], (B, M, D), jnp.float32)}
        for n, k in zip(['swq', 'swk', 'swv', 'swo'], jax.random.split(ks[2], 4)):
            inp[n] = jax.random.normal(k, (D, D), jnp.float32) * s
        for n in ['sbq', 'sbk', 'sbv', 'sbo']:
            inp[n] = jnp.zeros((D,), jnp.float32)
        for n, k in zip(['cwq', 'cwk', 'cwv', 'cwo'], jax.random.split(ks[3], 4)):
            inp[n] = jax.random.normal(k, (D, D), jnp.float32) * s
        for n in ['cbq', 'cbk', 'cbv', 'cbo']:
            inp[n] = jnp.zeros((D,), jnp.float32)
        inp['w1'] = jax.random.normal(ks[4], (D, FF), jnp.float32) * s
        inp['b1'] = jnp.zeros((FF,), jnp.float32)
        inp['w2'] = jax.random.normal(ks[5], (FF, D), jnp.float32) * s
        inp['b2'] = jnp.zeros((D,), jnp.float32)
        for n in ['g1', 'g2', 'g3']:
            inp[n] = jnp.ones((D,), jnp.float32)
        for n in ['be1', 'be2', 'be3']:
            inp[n] = jnp.zeros((D,), jnp.float32)
        return inp
    _L0_xattn_all = _L0_xattn_setup()
    _L0_xattn_in = {k: v for k, v in _L0_xattn_all.items() if k in ('swq', 'sbq', 'swk', 'sbk', 'swv', 'sbv', 'swo', 'sbo', 'cwq', 'cbq', 'cwk', 'cbk', 'cwv', 'cbv', 'cwo', 'cbo', 'w1', 'b1', 'w2', 'b2', 'g1', 'be1', 'g2', 'be2', 'g3', 'be3')}
    del _L0_xattn_all

    def _L1_xattn_setup():
        import jax, jax.numpy as jnp
        import numpy as np
        EPS = 1e-06
        N_HEADS = 16

        def rmsnorm(x, g):
            return x * jax.lax.rsqrt(jnp.mean(x * x, axis=-1, keepdims=True) + EPS) * g
        key = jax.random.key(seed)
        ks = jax.random.split(key, 8)
        B, Tq, Tc, dq, dc, dm = (2, 256, 256, 128, 128, 128)
        query = jax.random.normal(ks[0], (B, Tq, dq), dtype=jnp.float32)
        context = jax.random.normal(ks[1], (B, Tc, dc), dtype=jnp.float32)
        context_mask = jnp.ones((B, Tc), dtype=bool)
        s = 0.02
        Wq = jax.random.normal(ks[2], (dq, dm), dtype=jnp.float32) * s
        Wk = jax.random.normal(ks[3], (dc, dm), dtype=jnp.float32) * s
        Wv = jax.random.normal(ks[4], (dc, dm), dtype=jnp.float32) * s
        Wo = jax.random.normal(ks[5], (dm, dq), dtype=jnp.float32) * s
        g_q = jnp.ones((dq,), dtype=jnp.float32)
        g_c = jnp.ones((dc,), dtype=jnp.float32)
        g_out = jnp.ones((dq,), dtype=jnp.float32)
        return dict(query=query, context=context, context_mask=context_mask, Wq=Wq, Wk=Wk, Wv=Wv, Wo=Wo, g_q=g_q, g_c=g_c, g_out=g_out)
    _L1_xattn_all = _L1_xattn_setup()
    _L1_xattn_in = {k: v for k, v in _L1_xattn_all.items() if k in ('Wq', 'Wk', 'Wv', 'Wo', 'g_q', 'g_c', 'g_out')}
    del _L1_xattn_all
    return {'x': x, 'ctx_1024': ctx_1024, 'mask_BxS2_bf1': mask_BxS2_bf1, 'L0_xattn_swq': _L0_xattn_in['swq'], 'L0_xattn_sbq': _L0_xattn_in['sbq'], 'L0_xattn_swk': _L0_xattn_in['swk'], 'L0_xattn_sbk': _L0_xattn_in['sbk'], 'L0_xattn_swv': _L0_xattn_in['swv'], 'L0_xattn_sbv': _L0_xattn_in['sbv'], 'L0_xattn_swo': _L0_xattn_in['swo'], 'L0_xattn_sbo': _L0_xattn_in['sbo'], 'L0_xattn_cwq': _L0_xattn_in['cwq'], 'L0_xattn_cbq': _L0_xattn_in['cbq'], 'L0_xattn_cwk': _L0_xattn_in['cwk'], 'L0_xattn_cbk': _L0_xattn_in['cbk'], 'L0_xattn_cwv': _L0_xattn_in['cwv'], 'L0_xattn_cbv': _L0_xattn_in['cbv'], 'L0_xattn_cwo': _L0_xattn_in['cwo'], 'L0_xattn_cbo': _L0_xattn_in['cbo'], 'L0_xattn_w1': _L0_xattn_in['w1'], 'L0_xattn_b1': _L0_xattn_in['b1'], 'L0_xattn_w2': _L0_xattn_in['w2'], 'L0_xattn_b2': _L0_xattn_in['b2'], 'L0_xattn_g1': _L0_xattn_in['g1'], 'L0_xattn_be1': _L0_xattn_in['be1'], 'L0_xattn_g2': _L0_xattn_in['g2'], 'L0_xattn_be2': _L0_xattn_in['be2'], 'L0_xattn_g3': _L0_xattn_in['g3'], 'L0_xattn_be3': _L0_xattn_in['be3'], 'L1_xattn_Wq': _L1_xattn_in['Wq'], 'L1_xattn_Wk': _L1_xattn_in['Wk'], 'L1_xattn_Wv': _L1_xattn_in['Wv'], 'L1_xattn_Wo': _L1_xattn_in['Wo'], 'L1_xattn_g_q': _L1_xattn_in['g_q'], 'L1_xattn_g_c': _L1_xattn_in['g_c'], 'L1_xattn_g_out': _L1_xattn_in['g_out']}

def reference(x, ctx_1024, mask_BxS2_bf1, L0_xattn_swq, L0_xattn_sbq, L0_xattn_swk, L0_xattn_sbk, L0_xattn_swv, L0_xattn_sbv, L0_xattn_swo, L0_xattn_sbo, L0_xattn_cwq, L0_xattn_cbq, L0_xattn_cwk, L0_xattn_cbk, L0_xattn_cwv, L0_xattn_cbv, L0_xattn_cwo, L0_xattn_cbo, L0_xattn_w1, L0_xattn_b1, L0_xattn_w2, L0_xattn_b2, L0_xattn_g1, L0_xattn_be1, L0_xattn_g2, L0_xattn_be2, L0_xattn_g3, L0_xattn_be3, L1_xattn_Wq, L1_xattn_Wk, L1_xattn_Wv, L1_xattn_Wo, L1_xattn_g_q, L1_xattn_g_c, L1_xattn_g_out):
    import jax
    import jax.numpy as jnp

    def _L0_xattn_ref(x, mem, swq, sbq, swk, sbk, swv, sbv, swo, sbo, cwq, cbq, cwk, cbk, cwv, cbv, cwo, cbo, w1, b1, w2, b2, g1, be1, g2, be2, g3, be3):
        import jax, jax.numpy as jnp
        import numpy as np
        B, L, M, D, H, FF, W = (2, 256, 256, 128, 16, 512, 64)
        DH = D // H

        def _layernorm(x, g, b, eps=1e-05):
            mu = x.mean(-1, keepdims=True)
            var = ((x - mu) ** 2).mean(-1, keepdims=True)
            return (x - mu) / jnp.sqrt(var + eps) * g + b

        def _mha(qx, kx, wq, bq, wk, bk, wv, bv, wo, bo, mask, bias):
            Bq, Lq, _ = qx.shape
            Lk = kx.shape[1]
            q = (qx @ wq + bq).reshape(Bq, Lq, H, DH).transpose(0, 2, 1, 3)
            k = (kx @ wk + bk).reshape(Bq, Lk, H, DH).transpose(0, 2, 1, 3)
            v = (kx @ wv + bv).reshape(Bq, Lk, H, DH).transpose(0, 2, 1, 3)
            s = jnp.einsum('bhqd,bhkd->bhqk', q, k) / jnp.sqrt(jnp.asarray(DH, qx.dtype))
            if bias is not None:
                s = s + bias[None]
            if mask is not None:
                s = jnp.where(mask[None, None], s, jnp.asarray(-1000000000.0, qx.dtype))
            a = jax.nn.softmax(s, axis=-1)
            o = jnp.einsum('bhqk,bhkd->bhqd', a, v).transpose(0, 2, 1, 3).reshape(Bq, Lq, D)
            return o @ wo + bo

        def _forward(x, mem, swq, sbq, swk, sbk, swv, sbv, swo, sbo, cwq, cbq, cwk, cbk, cwv, cbv, cwo, cbo, w1, b1, w2, b2, g1, be1, g2, be2, g3, be3):
            i = jnp.arange(L)[:, None]
            j = jnp.arange(L)[None, :]
            mask = (j <= i) & (i - j < W)
            slopes = 2.0 ** (-8.0 * jnp.arange(1, H + 1, dtype=x.dtype) / H)
            bias = slopes[:, None, None] * (j - i).astype(x.dtype)[None]
            sa = _mha(x, x, swq, sbq, swk, sbk, swv, sbv, swo, sbo, mask, bias)
            x = _layernorm(x + sa, g1, be1)
            ca = _mha(x, mem, cwq, cbq, cwk, cbk, cwv, cbv, cwo, cbo, None, None)
            x = _layernorm(x + ca, g2, be2)
            ff = jax.nn.gelu(x @ w1 + b1, approximate=False) @ w2 + b2
            return _layernorm(x + ff, g3, be3)
        return _forward(x, mem, swq, sbq, swk, sbk, swv, sbv, swo, sbo, cwq, cbq, cwk, cbk, cwv, cbv, cwo, cbo, w1, b1, w2, b2, g1, be1, g2, be2, g3, be3)

    def _L1_xattn_ref(query, context, context_mask, Wq, Wk, Wv, Wo, g_q, g_c, g_out):
        import jax, jax.numpy as jnp
        import numpy as np
        EPS = 1e-06
        N_HEADS = 16

        def rmsnorm(x, g):
            return x * jax.lax.rsqrt(jnp.mean(x * x, axis=-1, keepdims=True) + EPS) * g
        B, Tq, _ = query.shape
        Tc = context.shape[1]
        H = N_HEADS
        dm = Wq.shape[1]
        hd = dm // H
        scale = hd ** (-0.5)
        q_norm = rmsnorm(query, g_q)
        c_norm = rmsnorm(context, g_c)
        Q = (q_norm @ Wq).reshape(B, Tq, H, hd).transpose(0, 2, 1, 3)
        K = (c_norm @ Wk).reshape(B, Tc, H, hd).transpose(0, 2, 1, 3)
        V = (c_norm @ Wv).reshape(B, Tc, H, hd).transpose(0, 2, 1, 3)
        scores = jnp.einsum('bhqd,bhkd->bhqk', Q, K) * scale
        scores = jnp.where(context_mask[:, None, None, :], scores, -jnp.inf)
        attn = jax.nn.softmax(scores, axis=-1)
        attn = jnp.nan_to_num(attn, nan=0.0)
        out = jnp.einsum('bhqk,bhkd->bhqd', attn, V)
        out = out.transpose(0, 2, 1, 3).reshape(B, Tq, dm)
        out = out @ Wo
        return rmsnorm(query + out, g_out)
    x = _L0_xattn_ref(x, ctx_1024, L0_xattn_swq, L0_xattn_sbq, L0_xattn_swk, L0_xattn_sbk, L0_xattn_swv, L0_xattn_sbv, L0_xattn_swo, L0_xattn_sbo, L0_xattn_cwq, L0_xattn_cbq, L0_xattn_cwk, L0_xattn_cbk, L0_xattn_cwv, L0_xattn_cbv, L0_xattn_cwo, L0_xattn_cbo, L0_xattn_w1, L0_xattn_b1, L0_xattn_w2, L0_xattn_b2, L0_xattn_g1, L0_xattn_be1, L0_xattn_g2, L0_xattn_be2, L0_xattn_g3, L0_xattn_be3)
    x = _L1_xattn_ref(x, ctx_1024, mask_BxS2_bf1, L1_xattn_Wq, L1_xattn_Wk, L1_xattn_Wv, L1_xattn_Wo, L1_xattn_g_q, L1_xattn_g_c, L1_xattn_g_out)
    return x

_drawn_inputs = setup_inputs


def setup_inputs(seed=0):
    import zlib

    import numpy as np

    out = dict(_drawn_inputs(seed))
    spreads = {'L0_xattn_sbq': (0.0, 0.8),
     'L0_xattn_sbk': (0.0, 2.0),
     'L0_xattn_sbv': (0.0, 0.37),
     'L0_xattn_sbo': (0.0, 0.1),
     'L0_xattn_cbq': (0.0, 2.0),
     'L0_xattn_cbk': (0.0, 2.0),
     'L0_xattn_cbv': (0.0, 0.396),
     'L0_xattn_cbo': (0.0, 0.1),
     'L0_xattn_b1': (0.0, 0.402),
     'L0_xattn_b2': (0.0, 0.1),
     'L0_xattn_g1': (1.0, 0.2),
     'L0_xattn_be1': (0.0, 0.1),
     'L0_xattn_g2': (1.0, 0.2),
     'L0_xattn_be2': (0.0, 0.1),
     'L0_xattn_g3': (1.0, 0.2),
     'L0_xattn_be3': (0.0, 0.1),
     'L1_xattn_g_q': (1.0, 0.6),
     'L1_xattn_g_c': (1.0, 0.6),
     'L1_xattn_g_out': (1.0, 0.2)}
    factors = {'L0_xattn_swq': 8.0,
     'L0_xattn_swk': 8.0,
     'L0_xattn_swv': 3.82,
     'L0_xattn_cwq': 8.0,
     'L0_xattn_cwk': 8.0,
     'L1_xattn_Wq': 8.0,
     'L1_xattn_Wk': 8.0}
    for name, (base, spread) in spreads.items():
        noise = np.random.default_rng([zlib.crc32(name.encode()), seed]).standard_normal(out[name].shape)
        drawn = base * np.exp(spread * noise) if base else spread * noise
        out[name] = jnp.asarray(drawn.astype(out[name].dtype))
    for name, factor in factors.items():
        out[name] = (out[name] * factor).astype(out[name].dtype)
    return out
```

```python
from contextlib import ExitStack

import numpy as np

import concourse.bass as bass
from concourse import mybir

ALU = mybir.AluOpType
ACT = mybir.ActivationFunctionType
AX = mybir.AxisListType
F32 = mybir.dt.float32
BF16 = mybir.dt.bfloat16
U8 = mybir.dt.uint8

B, LQ, LK, D, H, FF, WIN = 8, 256, 512, 128, 16, 512, 64
DH = D // H
P = 128
QT = LQ // P
CT_N = LK // P
BLK = WIN
NBLK = LQ // BLK
PAD = BLK
SCALE = float(DH) ** -0.5
NEG = -1.0e30
CAP = 1.0e20
TINY = 1.0e-30
LN_EPS, RMS_EPS = 1e-5, 1e-6

Q_PART = (0, 1, 2, 0, 1, 0)
K_PART = (0, 0, 0, 1, 1, 2)
NG = len(Q_PART)
ROW_X = 8 * NG
ROWS_MAX = 96
ROW_M = 96
ROWS_ALL = ROW_M + 3
QUADS = H // 4

KEYS = (LQ, LK, LK)
TILES = (QUADS, H, H)
MAXT = (QT * QUADS, QT * H, QT * H)

MISC = {
    0: {0: ("V", "XT", "CT"), 1: ("D", "Q"), 2: ("K", "O"), 3: ("MT",)},
    1: {4: ("V",), 5: ("XT",), 6: ("CT",), 7: ("D",), 8: ("Q",), 9: ("K",), 11: ("O",), 14: ("MT",)},
}
MISC[2] = MISC[1]
PV_LAG = 5
RAW_SLOT = (0, 5, 5)
NORM_SLOT = (3, 12, 12)
MAX_SLOTS = ((1, 2, 3), tuple(range(3, 14)), tuple(range(3, 14)))


class Unit:

    def __init__(self, stage, batch, parity):
        self.stage, self.batch, self.parity = stage, batch, parity

    def shift(self, d):
        if not isinstance(self.batch, int):
            return Unit(self.stage, self.batch + d, (self.parity + d) % 2)
        s, b = self.stage, self.batch + d
        if s == 0 and b >= B:
            s, b = 1, b - B
        elif s == 1 and b < 0:
            s, b = 0, b + B
        return Unit(s, b, b % 2) if 0 <= b < B else None


class PerUnit:

    def __init__(self, n0, n1=None, n2=None):
        self.n = (n0, n0 if n1 is None else n1, n0 if n2 is None else n2)

    def at(self, u, k):
        return sum(self.n[:u.stage]) * B + u.batch * self.n[u.stage] + k

    def whole(self, u):
        return self.at(u, self.n[u.stage])


ONE = PerUnit(1)
TWO = PerUnit(2)
FOUR = PerUnit(4)
SCORES = PerUnit(*TILES)
MAXIMA = PerUnit(*MAXT)
QUAD4 = PerUnit(QUADS)
STACKS = PerUnit(16 * (2 * NG + 1))
MROWS = PerUnit(16 * 3)
NORMS = PerUnit(4)


def schedule(eng, step, feed_forward):
    for stage in range(3):
        if stage != 1:
            step(Unit(stage, -2, 0), False)
            step(Unit(stage, -1, 1), False)
        step(Unit(stage, 0, 0), True)
        with eng.Fori(0, 2) as i:
            step(Unit(stage, i * 2 + 1, 1), True)
            step(Unit(stage, i * 2 + 2, 0), True)
        for b in (5, 6, 7):
            step(Unit(stage, b, b % 2), True)
        if stage == 1:
            step(Unit(stage, B, 0), False)
            feed_forward()
    step(Unit(2, B, 0), False)


def neighbours(u):
    if isinstance(u.batch, int) and not 0 <= u.batch < B:
        def near(d):
            b = u.batch + d
            return Unit(u.stage, b, b % 2) if 0 <= b < B else None
        return near(-1), near(1), near(2)
    return u.shift(-1), u.shift(1), u.shift(2)


def max_tasks(step_stage, u):
    slots = MAX_SLOTS[step_stage]
    n = MAXT[u.stage]
    return {s: range(n * i // len(slots), n * (i + 1) // len(slots)) for i, s in enumerate(slots)}


def wait(eng, sem, value):
    if not isinstance(value, int) or value > 0:
        eng.wait_ge(sem, value)


def two_layer_kernel(nc, a, out):
    with ExitStack() as ctx:
        def sb(name, shape, dt=F32):
            return ctx.enter_context(nc.sbuf_tensor(name, shape, dt))

        def sem(name):
            return ctx.enter_context(nc.semaphore(name))

        st = ctx.enter_context(nc.psum_tensor("st", [P, 2, 1024], F32))
        mx = ctx.enter_context(nc.psum_tensor("mx", [P, 2, 512], F32))
        pv = ctx.enter_context(nc.psum_tensor("pv", [P, 512], F32))
        misc = ctx.enter_context(nc.psum_tensor("misc", [P, 512], F32))
        misc_bf = misc[:, :].bitcast(BF16)

        kst = [sb(f"kst{i}", [P, H, LK], BF16) for i in range(2)]
        qst = [sb(f"qst{i}", [P, H, LQ], BF16) for i in range(2)]
        probs = sb("probs", [P, QUADS, 4 * 1024])
        vp = [sb(f"vp{i}", [P, 4, H, 32]) for i in range(2)]
        xs = sb("xs", [P, B, QT, D])
        xin = sb("xin", [P, QT, D])
        xn = sb("xn", [P, QT, D])
        cin = [sb(f"cin{i}", [P, CT_N, D]) for i in range(2)]
        cn = sb("cn", [P, CT_N, D])
        xT = sb("xT", [P, PAD + LQ])
        cT = sb("cT", [P, LK])
        qf, kf = sb("qf", [P, LQ]), sb("kf", [P, LK])
        qr, kr = sb("qr", [P, LQ]), sb("kr", [P, LK])
        qs, ks = sb("qs", [P, 3, LQ], BF16), sb("ks", [P, 3, LK], BF16)
        negmax = sb("negmax", [P, QT, H])
        mcap = sb("mcap", [P, QT, H])
        mrest = sb("mrest", [P, QT, H])
        msplit = sb("msplit", [P, QT, P], BF16)
        mT = sb("mT", [3 * H, LQ], BF16)
        raw = sb("raw", [P, 512])
        rden = sb("rden", [P, 512])
        att = sb("att", [P, 512])
        xb = sb("xb", [P, QT, D])
        y, z = sb("y", [P, CT_N, D]), sb("z", [P, CT_N, D])
        bst, bag = sb("bst", [P, 4, 6]), sb("bag", [P, 4, 2])
        sq = sb("sq", [P, D])
        ysum, yms, yrs = sb("ysum", [P, 4]), sb("yms", [P, 4]), sb("yrs", [P, 4])
        nsum, nms, nrs = sb("nsum", [P, 6]), sb("nms", [P, 6]), sb("nrs", [P, 6])
        zg = sb("zg", [P, CT_N, D])
        minushalf = sb("minushalf", [P, 8])
        xf, xfb = sb("xf", [P, 4, D]), sb("xfb", [P, 4, D])
        xfT = sb("xfT", [P, 512])
        hT = probs[:, 0, 0:4 * 512].rearrange("p (f n) -> p f n", f=4)

        ident = sb("ident", [P, P])
        identb = sb("identb", [P, P], BF16)
        mask_t = sb("mask_t", [P, LQ], BF16)
        mask_q = sb("mask_q", [P, QT, P], BF16)
        spread = sb("spread", [P, P])
        dentiny = sb("dentiny", [P, 1])
        win = sb("win", [P, 9, P])
        w = {n + str(s): win[:, 3 * s + i, :] for s in range(2) for i, n in enumerate("qkv")}
        w.update({n + "2": sb("w2" + n, [P, P])[:, :] for n in "qkv"})
        woall = sb("woall", [P, 3, 2, D])
        wo = [woall[:, s, :, :] for s in range(3)]
        w1, w2 = sb("w1", [P, FF]), sb("w2", [P, FF // P, D])
        cols = sb("cols", [P, 14])
        bvab = [cols[:, 10 + 2 * s:12 + 2 * s] for s in range(2)]
        bvb = sb("bvb", [P, 2, 2, P])
        zero = sb("zero", [P, P])
        bo2 = [sb(f"bo2{s}", [P, D]) for s in range(2)]
        rows = sb("rows", [P, 10, D])
        bob = [rows[:, s, :] for s in range(2)]
        b2b = rows[:, 2, :]
        gam = [rows[:, 3 + i, :] for i in range(4)]
        bet = [rows[:, 7 + i, :] for i in range(3)]
        kmu = sb("kmu", [B, LK], U8)
        kmask = sb("kmask", [B, LK], BF16)

        qd = nc.dram_tensor("q_parts", [P, 3, LQ], BF16).ap()
        kd = nc.dram_tensor("k_parts", [P, 3, LK], BF16).ap()
        kmd = nc.dram_tensor("key_mask_rows", [B, LK], BF16).ap()
        qd_rows = qd.rearrange("(h d) s q -> d s h q", d=DH)
        kd_rows = kd.rearrange("(h d) s q -> d s h q", d=DH)

        consts_loaded = sem("consts_loaded")
        x_loaded = sem("x_loaded")
        stack_consts = sem("stack_consts")
        mask_loaded = sem("mask_loaded")
        mask_made = sem("mask_made")
        mask_stored = sem("mask_stored")
        dve_set, pool_set = sem("dve_set"), sem("pool_set")
        ones_set = sem("ones_set")
        weights_made = sem("weights_made")
        bias_product = sem("bias_product")
        bias_made = sem("bias_made")
        ctx_loaded = [sem("ctx_loaded0"), sem("ctx_loaded1")]
        x_copied = sem("x_copied")
        squares_summed = sem("squares_summed")
        means_made = sem("means_made")
        inputs_normed = sem("inputs_normed")
        ready = {n: sem("ready_" + n) for n in ("V", "XT", "CT", "D", "Q", "K", "O", "MT")}
        taken = {n: sem("taken_" + n) for n in ("V", "XT", "CT", "D", "Q", "K", "O", "MT")}
        q_steps, k_steps = sem("q_steps"), sem("k_steps")
        parts_stored = sem("parts_stored")
        stacks_loaded = sem("stacks_loaded")
        m_steps = sem("m_steps")
        mrows_loaded = sem("mrows_loaded")
        scores_ready = sem("scores_ready")
        exp_done = sem("exp_done")
        pv_done = sem("pv_done")
        maxin_ready = sem("maxin_ready")
        max_done = sem("max_done")
        raw_ready = sem("raw_ready")
        att_ready = sem("att_ready")
        xb_ready = sem("xb_ready")
        norm_steps = sem("norm_steps")
        stats_ready = sem("stats_ready")
        rs_steps = sem("rs_steps")
        normed = sem("normed")
        affine_steps = sem("affine_steps")
        x_ready = sem("x_ready")
        out_stored = sem("out_stored")
        f_copied, f_ready, f_T = sem("f_copied"), sem("f_ready"), sem("f_T")
        f_hidden, f_gelu, f_out, f_y = sem("f_hidden"), sem("f_gelu"), sem("f_out"), sem("f_y")
        f_xb = sem("f_xb")
        waits_passed = sem("waits_passed")
        f_stats, f_rs, f_normed, f_aff, f_x = (
            sem("f_stats"), sem("f_rs"), sem("f_normed"), sem("f_aff"), sem("f_x"))

        DVE_SETS, POOL_SETS = 7, 5

        def alone(eng):
            eng.sem_inc(waits_passed, 1)

        block = ctx.enter_context(nc.Block())

        def const_loads():
            yield ident[:, :], a["c_ident"]
            yield identb[:, :], a["c_identb"]
            yield mask_t[:, :], a["c_mask_t"]
            yield mask_q[:, :, :], a["c_mask_q"]
            yield spread[:, :], a["c_spread"]
            yield dentiny[:, :], a["c_dentiny"]
            yield win[:, :, :], a["w_in"]
            yield woall[:, :, :, :], a["w_out"]
            yield w1[:, :], a["L0_xattn_w1"]
            yield w2[:, :, :], a["L0_xattn_w2"].rearrange("(f p) d -> p f d", p=P)
            yield cols[:, :], a["columns"]
            yield rows[:, :, :], a["vectors"].rearrange("(o v) d -> o v d", o=1).to_broadcast([P, 10, D])

        CONSTS = 16 * len(list(const_loads()))

        def ctx_index(u):
            return (u.stage - 1) * B + u.batch

        def ctx_value(u):
            if isinstance(u.batch, int):
                return 16 * ((u.stage - 1) * (B // 2) + u.batch // 2 + 1)
            return ((u.stage - 1) * (B // 2) + 1) * 16 + (u.batch - u.parity) * 8

        @block.sync
        def _(sp):
            sp.dma_start(xs[:, :, :, :], a["x"].rearrange("b (t p) d -> p b t d", p=P)).then_inc(x_loaded, 16)
            for dst, src in const_loads():
                sp.dma_start(dst, src).then_inc(consts_loaded, 16)
            sp.dma_start(kmu[:, :], a["mask_BxS2_bf1"]).then_inc(mask_loaded, 16)
            sp.wait_ge(pool_set, POOL_SETS)
            for i in range(2):
                sp.dma_start(qst[i][ROW_X:ROW_X + 3, :, :], a["c_ones"]).then_inc(stack_consts, 16)
            sp.wait_ge(mask_made, 2)
            sp.dma_start(kmd, kmask[:, :]).then_inc(mask_stored, 16)
            sp.wait_ge(mask_stored, 16)

            def load_context(u):
                if u is None or u.stage == 0:
                    return
                if not (isinstance(u.batch, int) and u.stage == 1 and u.batch < 2):
                    wait(sp, ready["CT"], ctx_index(u) - 1)
                    if u.stage == 2:
                        if isinstance(u.batch, int):
                            wait(sp, inputs_normed, u.batch - 1)
                        else:
                            sp.wait_ge(inputs_normed, u.batch - 1)
                sp.dma_start(cin[u.parity][:, :, :],
                             a["ctx_1024"][u.batch].rearrange("(t p) d -> p t d", p=P)
                             ).then_inc(ctx_loaded[u.parity], 16)

            def step(u, main):
                before, nxt, nxt2 = neighbours(u)
                if not main and u.batch == -2:
                    load_context(nxt2)
                if nxt2 is not None:
                    n = nxt2
                    nk = KEYS[n.stage]
                    if not (isinstance(n.batch, int) and n.stage == 0 and n.batch == 0):
                        wait(sp, stacks_loaded, STACKS.at(n, 0))
                    sp.wait_ge(q_steps, FOUR.whole(n))
                    sp.dma_start(qd, qs[:, :, :]).then_inc(parts_stored, 16)
                    sp.wait_ge(k_steps, FOUR.whole(n))
                    sp.dma_start(kd[:, :, 0:nk], ks[:, :, 0:nk]).then_inc(parts_stored, 16)
                if nxt is not None:
                    sp.wait_ge(taken["MT"], ONE.whole(nxt))
                    for s in range(3):
                        sp.dma_start(qst[nxt.parity][ROW_M + s:ROW_M + s + 1, :, :],
                                     mT[s * H:(s + 1) * H, :]).then_inc(mrows_loaded, 16)
                if before is not None and before.stage == 2:
                    sp.wait_ge(affine_steps, ONE.whole(before))
                    sp.dma_start(out[before.batch].rearrange("(t p) d -> p t d", p=P),
                                 zg[:, 0:QT, :]).then_inc(out_stored, 16)
                if nxt2 is not None:
                    sp.wait_ge(parts_stored, PerUnit(32).whole(n))
                    if main:
                        sp.wait_ge(scores_ready, SCORES.whole(u))
                    col = PAD if n.stage == 0 else 0
                    for g in range(NG):
                        sp.dma_start(qst[n.parity][8 * g:8 * g + 8, :, :],
                                     qd_rows[:, Q_PART[g], :, :]).then_inc(stacks_loaded, 16)
                        sp.dma_start(kst[n.parity][8 * g:8 * g + 8, :, col:col + nk],
                                     kd_rows[:, K_PART[g], :, 0:nk]).then_inc(stacks_loaded, 16)
                    extra = kst[n.parity][ROW_X:ROW_X + 3, :, :]
                    if n.stage == 0:
                        sp.dma_start(extra[:, :, 0:PAD + LQ], a["c_slopes"]).then_inc(stacks_loaded, 16)
                    elif n.stage == 1:
                        sp.dma_start(extra, a["c_zeros"]).then_inc(stacks_loaded, 16)
                    else:
                        src = kmd[n.batch].rearrange("(o p k) -> o p k", o=1, p=1)
                        sp.dma_start(extra[0:1, :, :], src.to_broadcast([1, H, LK])
                                     ).then_inc(stacks_loaded, 16)
                load_context(nxt2.shift(1) if nxt2 is not None and nxt2.shift(1) is not None else None)

            def feed_forward():
                pass

            schedule(sp, step, feed_forward)
            sp.wait_ge(out_stored, 16 * B)

        @block.tensor
        def _(pe):
            pe.wait_ge(consts_loaded, CONSTS)
            pe.wait_ge(weights_made, 5)
            pe.wait_ge(bias_made, 4)
            for s in range(2):
                for r in range(2):
                    mm = nc.tensor.matmul(misc[:, s * D:(s + 1) * D], bvb[:, s, r, :], wo[s][:, r, :],
                                          start=(r == 0), stop=(r == 1))
            mm.then_inc(bias_product, 1)
            pe.wait_ge(bias_made, 6)
            pe.wait_ge(dve_set, DVE_SETS)
            pe.wait_ge(pool_set, POOL_SETS)
            pe.wait_ge(ones_set, 2)
            pe.wait_ge(stack_consts, 32)

            def scores(u, t):
                if t == 0:
                    pe.wait_ge(mrows_loaded, MROWS.whole(u))
                wait(pe, exp_done, SCORES.at(u, t - 1))
                dst = st[:, t % 2, :]
                k, q = kst[u.parity], qst[u.parity]
                if u.stage == 0:
                    for half in range(2):
                        nc.tensor.matmul(dst[:, 512 * half:512 * half + 512].rearrange("p (h q) -> p h q", h=2),
                                         identb[:, :],
                                         mask_t[:, :].rearrange("p (o q) -> p o q", o=1).to_broadcast([P, 2, LQ]),
                                         start=True, stop=False, skip_group_check=True)
                        for j in (2 * half, 2 * half + 1):
                            for c in range(NBLK):
                                at = j * LQ + c * BLK
                                mm = nc.tensor.matmul(
                                    dst[:, at:at + BLK],
                                    k[0:ROWS_ALL, 4 * t + j, c * BLK:c * BLK + 2 * BLK],
                                    q[0:ROWS_ALL, 4 * t + j, c * BLK:(c + 1) * BLK],
                                    start=False, stop=(c == NBLK - 1), skip_group_check=True)
                else:
                    for c in range(CT_N):
                        mm = nc.tensor.matmul(dst[:, c * LQ:(c + 1) * LQ],
                                              k[0:ROWS_ALL, t, c * P:(c + 1) * P],
                                              q[0:ROWS_ALL, t, :], start=True, stop=True)
                mm.then_inc(scores_ready, 1)

            def max_scores(u, n):
                if n == 0:
                    pe.wait_ge(stacks_loaded, STACKS.whole(u))
                wait(pe, max_done, MAXIMA.at(u, n - 1))
                dst = mx[:, n % 2, :]
                k, q = kst[u.parity], qst[u.parity]
                if u.stage == 0:
                    tile, quad = n % QT, n // QT
                    nc.tensor.matmul(dst.rearrange("p (h k) -> p h k", h=4), identb[:, :],
                                     mask_q[:, tile:tile + 1, :].to_broadcast([P, 4, P]),
                                     start=True, stop=False, skip_group_check=True)
                    for j in range(4):
                        for half in range(2):
                            c = 2 * tile + half
                            mm = nc.tensor.matmul(
                                dst[BLK * half:BLK * half + BLK, j * P:(j + 1) * P],
                                q[0:ROWS_MAX, 4 * quad + j, c * BLK:(c + 1) * BLK],
                                k[0:ROWS_MAX, 4 * quad + j, c * BLK:c * BLK + 2 * BLK],
                                start=False, stop=(j == 3), skip_group_check=True)
                else:
                    tile, head = n % QT, n // QT
                    mm = nc.tensor.matmul(dst, q[0:ROWS_MAX, head, tile * P:(tile + 1) * P],
                                          k[0:ROWS_MAX, head, :], start=True, stop=True)
                mm.then_inc(maxin_ready, 1)

            def weighted_values(u, quad, c):
                if c == 0:
                    last = quad + 1 if u.stage == 0 else 4 * quad + 4
                    pe.wait_ge(exp_done, SCORES.at(u, last))
                    if quad == 0:
                        pe.wait_ge(taken["V"], ONE.whole(u))
                        wait(pe, raw_ready, ONE.at(u, 0))
                region = quad // 2
                n = BLK if u.stage == 0 else LQ
                for j in range(4):
                    src = j * 4 * n + c * n
                    dst = region * LQ + (c * BLK if u.stage == 0 else 0)
                    mm = nc.tensor.matmul(pv[32 * j:32 * j + 32, dst:dst + n], vp[u.parity][:, c, 4 * quad + j, :],
                                          probs[:, quad, src:src + n], start=(quad == 0 and c == 0),
                                          stop=(quad == QUADS - 1 and c == 3), skip_group_check=True)
                if c == 3:
                    mm.then_inc(pv_done, 1)

            def small(name, u):
                s = u.stage
                if name == "V":
                    for c in range(4):
                        src = xT[:, c * BLK:c * BLK + P] if s == 0 else cT[:, c * P:(c + 1) * P]
                        mm = nc.tensor.matmul(misc[:, c * P:(c + 1) * P], src, w[f"v{s}"],
                                              start=True, stop=True)
                elif name == "XT":
                    if s == 2:
                        pe.wait_ge(inputs_normed, u.batch + 1)
                    else:
                        pe.wait_ge(x_copied, ONE.whole(u))
                    src = xn if s == 2 else xin
                    for t in range(QT):
                        mm = nc.tensor.transpose(misc[:, t * P:(t + 1) * P], src[:, t, :], ident[:, :])
                elif name == "CT":
                    if s == 1:
                        pe.wait_ge(ctx_loaded[u.parity], ctx_value(u))
                    src = cn if s == 2 else cin[u.parity]
                    for t in range(CT_N):
                        mm = nc.tensor.transpose(misc[:, t * P:(t + 1) * P], src[:, t, :], ident[:, :])
                elif name == "D":
                    pe.wait_ge(raw_ready, ONE.whole(u))
                    mm = nc.tensor.matmul(misc[:, :], spread[:, :], raw[:, :], start=True, stop=True)
                elif name == "Q":
                    pe.wait_ge(taken["XT"], ONE.whole(u))
                    mm = nc.tensor.matmul(misc[:, 0:LQ], w[f"q{s}"], xT[:, PAD:PAD + LQ],
                                          start=True, stop=True)
                elif name == "K":
                    src = xT[:, PAD:PAD + LQ] if s == 0 else cT[:, :]
                    if s > 0:
                        pe.wait_ge(taken["CT"], ctx_index(u) + 1)
                    mm = nc.tensor.matmul(misc[:, 0:KEYS[s]], w[f"k{s}"], src, start=True, stop=True)
                elif name == "O":
                    pe.wait_ge(att_ready, ONE.whole(u))
                    for t in range(QT):
                        for r in range(2):
                            at = r * LQ + t * P
                            mm = nc.tensor.matmul(misc[:, t * D:(t + 1) * D], att[:, at:at + P],
                                                  wo[s][:, r, :], start=(r == 0), stop=(r == 1))
                elif name == "MT":
                    pe.wait_ge(m_steps, PerUnit(5).whole(u))
                    for t in range(QT):
                        mm = nc.tensor.transpose(misc_bf[:, t * P:(t + 1) * P], msplit[:, t, :], identb[:, :])
                mm.then_inc(ready[name], 1)

            def step(u, main):
                before, nxt, nxt2 = neighbours(u)
                unit_of = {"V": nxt, "XT": nxt2, "CT": nxt2, "D": before, "Q": nxt2, "K": nxt2,
                           "O": before, "MT": nxt}
                last = ("MT", u) if main else last_of_step[0]
                tasks = max_tasks(u.stage, nxt) if nxt is not None else {}
                for t in range(TILES[u.stage]):
                    if main:
                        scores(u, t)
                    todo = list(tasks.get(t, ()))
                    for n in todo[:len(todo) // 2]:
                        max_scores(nxt, n)
                    if u.stage == 0:
                        if t == 0 and before is not None:
                            for c in range(4):
                                weighted_values(before, QUADS - 1, c)
                        elif t > 0 and main:
                            for c in range(4):
                                weighted_values(u, t - 1, c)
                    else:
                        if before is not None and before.stage > 0 and t < PV_LAG:
                            chunk = H - PV_LAG + t
                            weighted_values(before, chunk // 4, chunk % 4)
                        elif before is not None and before.stage == 0 and t == 0:
                            for c in range(4):
                                weighted_values(before, QUADS - 1, c)
                        if main and t >= PV_LAG:
                            weighted_values(u, (t - PV_LAG) // 4, (t - PV_LAG) % 4)
                    for n in todo[len(todo) // 2:]:
                        max_scores(nxt, n)
                    for name in MISC[u.stage].get(t, ()):
                        v = unit_of[name]
                        if v is None or (name == "CT" and v.stage == 0):
                            continue
                        if last is not None:
                            value = ctx_index(last[1]) + 1 if last[0] == "CT" else ONE.whole(last[1])
                            pe.wait_ge(taken[last[0]], value)
                        small(name, v)
                        last = (name, v)
                last_of_step[0] = last

            last_of_step = [None]

            def feed_forward():
                pe.sem_inc(f_ready, 1)
                pe.sem_inc(f_out, 1)
                with pe.Fori(0, 4) as i:
                    pe.wait_ge(f_copied, i + 1)
                    pe.wait_ge(f_y, i + 1)
                    for t in range(4):
                        mm = nc.tensor.transpose(mx[:, 0, t * P:(t + 1) * P], xf[:, t, :], ident[:, :])
                    mm.then_inc(f_ready, 1)
                    pe.wait_ge(f_T, i + 1)
                    for f in range(4):
                        nc.tensor.matmul(st[:, f // 2, (f % 2) * 512:(f % 2) * 512 + 512],
                                         w1[:, f * P:(f + 1) * P], xfT[:, :], start=True, stop=True
                                         ).then_inc(f_hidden, 1)
                    for t in range(4):
                        for f in range(4):
                            if t == 0:
                                pe.wait_ge(f_gelu, i * 4 + f + 1)
                            mm = nc.tensor.matmul(mx[:, 1, t * D:(t + 1) * D], hT[:, f, t * P:(t + 1) * P],
                                                  w2[:, f, :], start=(f == 0), stop=(f == 3))
                    mm.then_inc(f_out, 1)
                last_of_step[0] = None

            schedule(pe, step, feed_forward)

        @block.scalar
        def _(act):
            act.wait_ge(consts_loaded, CONSTS)
            act.wait_ge(dve_set, DVE_SETS)
            act.wait_ge(ones_set, 2)

            def take(name, u):
                s = u.stage
                if name == "V":
                    act.wait_ge(ready["V"], ONE.whole(u))
                    wait(act, pv_done, QUAD4.at(u, -QUADS))
                    for gg in range(2):
                        for r in range(2):
                            heads = slice(4 * (2 * r + gg), 4 * (2 * r + gg) + 4)
                            ins = nc.scalar.copy(
                                vp[u.parity][:, :, heads, 16 * gg:16 * gg + DH],
                                misc[:, :].rearrange("p (c h d) -> p c h d", c=4, h=H)[:, :, heads, :])
                    ins.then_inc(taken["V"], 1)
                elif name == "CT":
                    act.wait_ge(ready["CT"], ctx_index(u) + 1)
                    nc.scalar.copy(cT[:, :], misc[:, :]).then_inc(taken["CT"], 1)
                elif name in ("Q", "K"):
                    n = LQ if name == "Q" else KEYS[s]
                    dst = qf if name == "Q" else kf
                    act.wait_ge(ready[name], ONE.whole(u))
                    wait(act, q_steps if name == "Q" else k_steps, FOUR.at(u, 0))
                    if s == 2:
                        ins = nc.scalar.copy(dst[:, 0:n], misc[:, 0:n])
                    else:
                        col = 2 * s + (name == "K")
                        ins = nc.scalar.activation(dst[:, 0:n], misc[:, 0:n], ACT.Identity,
                                                   bias=cols[:, col:col + 1])
                    ins.then_inc(taken[name], 1)

            def step(u, main):
                before, nxt, nxt2 = neighbours(u)
                unit_of = {"V": nxt, "CT": nxt2, "Q": nxt2, "K": nxt2}
                for t in range(TILES[u.stage]):
                    if main:
                        act.wait_ge(scores_ready, SCORES.at(u, t + 1))
                        quad, j = (t, 0) if u.stage == 0 else (t // 4, t % 4)
                        if j == 0:
                            wait(act, pv_done, QUAD4.at(u, quad + 1 - QUADS))
                        nc.scalar.activation(probs[:, quad, j * 1024:(j + 1) * 1024], st[:, t % 2, :],
                                             ACT.Exp, scale=SCALE).then_inc(exp_done, 1)
                    for name in MISC[u.stage].get(t, ()):
                        v = unit_of.get(name)
                        if v is not None and not (name == "CT" and v.stage == 0):
                            take(name, v)

            def feed_forward():
                with act.Fori(0, 4) as i:
                    act.wait_ge(f_out, i + 1)
                    for f in range(4):
                        act.wait_ge(f_hidden, i * 4 + f + 1)
                        nc.scalar.activation(hT[:, f, :], st[:, f // 2, (f % 2) * 512:(f % 2) * 512 + 512],
                                             ACT.Gelu, bias=cols[:, 6 + f:7 + f]).then_inc(f_gelu, 1)

            schedule(act, step, feed_forward)

        @block.vector
        def _(dve):
            for i in range(2):
                nc.vector.memset(kst[i][0:ROWS_MAX, :, :].bitcast(mybir.dt.uint32), 0).then_inc(dve_set, 1)
                nc.vector.memset(vp[i][:, :, :, :], 0.0).then_inc(dve_set, 1)
            nc.vector.memset(xT[:, 0:PAD], 0.0).then_inc(dve_set, 1)
            nc.vector.memset(minushalf[:, :], -0.5).then_inc(dve_set, 1)
            nc.vector.memset(zero[:, :], 0.0).then_inc(dve_set, 1)
            dve.wait_ge(mask_loaded, 16)
            nc.vector.tensor_scalar(kmask[:, :], kmu[:, :], -NEG, NEG, ALU.mult, ALU.add).then_inc(mask_made, 2)
            dve.wait_ge(consts_loaded, CONSTS)
            for i, (n, col) in enumerate((("q2", 4), ("k2", 5), ("v2", 5))):
                nc.vector.tensor_scalar(w[n], win[:, 6 + i, :], cols[:, col:col + 1], None, ALU.mult
                                        ).then_inc(weights_made, 1)
            dve.wait_ge(dve_set, DVE_SETS)
            dve.wait_ge(pool_set, POOL_SETS)
            for i in range(2):
                nc.vector.memset(kst[i][ROW_M:ROWS_ALL, :, :], 1.0).then_inc(weights_made, 1)
                for gg in range(2):
                    for r in range(2):
                        heads = slice(4 * (2 * r + gg), 4 * (2 * r + gg) + 4)
                        ins = nc.vector.memset(vp[i][:, :, heads, 16 * gg + DH:16 * gg + 2 * DH], 1.0)
                ins.then_inc(ones_set, 1)
            for s in range(2):
                for r in range(2):
                    nc.vector.tensor_scalar(bvb[:, s, r, :], zero[:, :], bvab[s][:, r:r + 1], None,
                                            ALU.add).then_inc(bias_made, 1)
            dve.wait_ge(bias_product, 1)
            for s in range(2):
                nc.vector.tensor_tensor(bo2[s][:, :], misc[:, s * D:(s + 1) * D], bob[s], ALU.add
                                        ).then_inc(bias_made, 1)

            def maximum(u, n):
                dve.wait_ge(maxin_ready, MAXIMA.at(u, n + 1))
                if n == 0:
                    wait(dve, m_steps, PerUnit(5).at(u, 0))
                tile = n % QT
                if u.stage == 0:
                    quad = n // QT
                    ins = nc.vector.tensor_reduce(negmax[:, tile, 4 * quad:4 * quad + 4],
                                                  mx[:, n % 2, :].rearrange("p (h k) -> p h k", h=4),
                                                  AX.X, ALU.max, negate=True)
                else:
                    ins = nc.vector.tensor_reduce(negmax[:, tile, n // QT:n // QT + 1], mx[:, n % 2, :],
                                                  AX.X, ALU.max, negate=True)
                ins.then_inc(max_done, 1)

            def split_maxima(u):
                steps = PerUnit(5)
                dve.wait_ge(max_done, MAXIMA.whole(u))
                wait(dve, ready["MT"], ONE.at(u, 0))
                nc.vector.tensor_scalar(mcap[:, :, :], negmax[:, :, :], CAP, None, ALU.min).then_inc(m_steps, 1)
                nc.vector.tensor_scalar(msplit[:, :, 0:H], negmax[:, :, :], CAP, None, ALU.min).then_inc(m_steps, 1)
                dve.wait_ge(m_steps, steps.at(u, 2))
                nc.vector.tensor_tensor(mrest[:, :, :], mcap[:, :, :], msplit[:, :, 0:H], ALU.subtract
                                        ).then_inc(m_steps, 1)
                dve.wait_ge(m_steps, steps.at(u, 3))
                nc.vector.tensor_copy(msplit[:, :, H:2 * H], mrest[:, :, :]).then_inc(m_steps, 1)
                dve.wait_ge(m_steps, steps.at(u, 4))
                nc.vector.tensor_tensor(msplit[:, :, 2 * H:3 * H], mrest[:, :, :], msplit[:, :, H:2 * H], ALU.subtract
                                        ).then_inc(m_steps, 1)

            def take(name, u):
                if name == "XT":
                    dve.wait_ge(ready["XT"], ONE.whole(u))
                    nc.vector.tensor_copy(xT[:, PAD:PAD + LQ], misc[:, 0:LQ]).then_inc(taken["XT"], 1)
                elif name == "D":
                    dve.wait_ge(ready["D"], ONE.whole(u))
                    wait(dve, att_ready, ONE.at(u, 0))
                    nc.vector.reciprocal(rden[:, :], misc[:, :]).then_inc(taken["D"], 1)
                elif name == "O":
                    dve.wait_ge(ready["O"], ONE.whole(u))
                    dve.wait_ge(xb_ready, ONE.whole(u))
                    nc.vector.tensor_tensor(y[:, 0:QT, :].rearrange("p t d -> p (t d)"), misc[:, 0:QT * D],
                                            xb[:, :, :].rearrange("p t d -> p (t d)"), ALU.add
                                            ).then_inc(taken["O"], 1)
                    dve.wait_ge(taken["O"], ONE.whole(u))
                    if u.stage < 2:
                        for t in range(QT):
                            nc.vector.bn_stats(bst[:, t, :], y[:, t, :]).then_inc(norm_steps, 1)
                        for t in range(QT):
                            dve.wait_ge(norm_steps, TWO.at(u, t + 1))
                            alone(dve)
                            nc.vector.bn_aggr(bag[:, t, :], bst[:, t, :]).then_inc(stats_ready, 1)
                    else:
                        for t in range(QT):
                            if t:
                                dve.wait_ge(norm_steps, TWO.at(u, t))
                            nc.vector.tensor_tensor_reduce(sq[:, :], y[:, t, :], y[:, t, :], 1.0, 0.0,
                                                           ALU.mult, ALU.add, ysum[:, t:t + 1]
                                                           ).then_inc(norm_steps, 1)
                elif name == "MT":
                    dve.wait_ge(ready["MT"], ONE.whole(u))
                    wait(dve, mrows_loaded, MROWS.at(u, 0))
                    nc.vector.tensor_copy(mT[:, :], misc_bf[0:3 * H, 0:LQ]).then_inc(taken["MT"], 1)

            def take_raw(u):
                dve.wait_ge(pv_done, QUAD4.whole(u))
                wait(dve, att_ready, ONE.at(u, 0))
                nc.vector.tensor_scalar(raw[:, :], pv[:, :], dentiny[:, 0:1], None, ALU.add
                                        ).then_inc(raw_ready, 1)

            def apply_norm(u):
                dve.wait_ge(rs_steps, TWO.whole(u))
                wait(dve, affine_steps, ONE.at(u, 0))
                for t in range(QT):
                    if u.stage < 2:
                        ins = nc.vector.tensor_scalar(z[:, t, :], y[:, t, :], bag[:, t, 0:1], yrs[:, t:t + 1],
                                                      ALU.subtract, ALU.mult)
                    else:
                        ins = nc.vector.tensor_scalar(z[:, t, :], y[:, t, :], yrs[:, t:t + 1], None, ALU.mult)
                    ins.then_inc(normed, 1)

            def square_inputs(u):
                dve.wait_ge(x_copied, ONE.whole(u))
                dve.wait_ge(ctx_loaded[u.parity], ctx_value(u))
                for t in range(QT + CT_N):
                    src = xin[:, t, :] if t < QT else cin[u.parity][:, t - QT, :]
                    wait(dve, squares_summed, PerUnit(0, 0, QT + CT_N).at(u, t))
                    nc.vector.tensor_tensor_reduce(sq[:, :], src, src, 1.0, 0.0, ALU.mult, ALU.add,
                                                   nsum[:, t:t + 1]).then_inc(squares_summed, 1)

            def step(u, main):
                before, nxt, nxt2 = neighbours(u)
                unit_of = {"XT": nxt2, "D": before, "O": before, "MT": nxt}
                tasks = max_tasks(u.stage, nxt) if nxt is not None else {}
                if nxt2 is not None and nxt2.stage == 2:
                    square_inputs(nxt2)
                for t in range(TILES[u.stage]):
                    names = MISC[u.stage].get(t, ())
                    if t == RAW_SLOT[u.stage] and before is not None:
                        take_raw(before)
                    for n in tasks.get(t, ()):
                        maximum(nxt, n)
                    if nxt is not None and t == MAX_SLOTS[u.stage][-1]:
                        split_maxima(nxt)
                    if before is not None and t == NORM_SLOT[u.stage]:
                        apply_norm(before)
                    for name in names:
                        v = unit_of.get(name)
                        if v is not None:
                            take(name, v)

            def feed_forward():
                dve.sem_inc(f_y, 1)
                with dve.Fori(0, 4) as i:
                    dve.wait_ge(f_ready, i + 2)
                    nc.vector.tensor_copy(xfT[:, :], mx[:, 0, :]).then_inc(f_T, 1)
                    dve.wait_ge(f_out, i + 2)
                    dve.wait_ge(f_xb, i + 1)
                    nc.vector.tensor_tensor(y[:, :, :].rearrange("p t d -> p (t d)"), mx[:, 1, :],
                                            xfb[:, :, :].rearrange("p t d -> p (t d)"), ALU.add
                                            ).then_inc(f_y, 1)
                    dve.wait_ge(f_y, i + 2)
                    for t in range(4):
                        nc.vector.bn_stats(bst[:, t, :], y[:, t, :]).then_inc(f_stats, 1)
                    for t in range(4):
                        dve.wait_ge(f_stats, i * 8 + 4)
                        alone(dve)
                        nc.vector.bn_aggr(bag[:, t, :], bst[:, t, :]).then_inc(f_stats, 1)
                    dve.wait_ge(f_rs, i * 2 + 2)
                    for t in range(4):
                        nc.vector.tensor_scalar(z[:, t, :], y[:, t, :], bag[:, t, 0:1], yrs[:, t:t + 1],
                                                ALU.subtract, ALU.mult).then_inc(f_normed, 1)

            schedule(dve, step, feed_forward)

        @block.gpsimd
        def _(pool):
            for i in range(2):
                nc.gpsimd.memset(qst[i][0:ROWS_MAX, :, :], 0.0).then_inc(pool_set, 1)
            nc.gpsimd.memset(bst[:, :, :], 0.0).then_inc(pool_set, 1)
            nc.gpsimd.memset(msplit[:, :, :], 0.0).then_inc(pool_set, 1)
            nc.gpsimd.memset(zg[:, :, :], 0.0).then_inc(pool_set, 1)
            pool.wait_ge(x_loaded, 16)
            pool.wait_ge(dve_set, DVE_SETS)
            pool.wait_ge(pool_set, POOL_SETS)
            pool.wait_ge(bias_made, 6)
            pool.wait_ge(consts_loaded, CONSTS)

            def rows_of(t, n):
                return t.rearrange("p (o d) -> p o d", o=1).to_broadcast([P, n, D])

            def copy_input(u):
                if u.stage == 1:
                    pool.wait_ge(x_ready, u.batch + 1)
                elif u.stage == 2:
                    pool.wait_ge(f_x, 4)
                wait(pool, ready["XT"], ONE.at(u, 0))
                alone(pool)
                nc.gpsimd.tensor_copy(xin[:, :, :], xs[:, u.batch, :, :]).then_inc(x_copied, 1)

            def norm_inputs(u):
                squares = PerUnit(0, 0, QT + CT_N)
                pool.wait_ge(squares_summed, squares.whole(u))
                alone(pool)
                nc.gpsimd.tensor_scalar(nms[:, :], nsum[:, :], 1.0 / D, RMS_EPS, ALU.mult, ALU.add
                                        ).then_inc(means_made, 1)
                pool.wait_ge(means_made, PerUnit(0, 0, 2).at(u, 1))
                nc.gpsimd.tensor_tensor(nrs[:, :], nms[:, :], minushalf[:, 0:QT + CT_N], ALU.pow
                                        ).then_inc(means_made, 1)
                pool.wait_ge(means_made, PerUnit(0, 0, 2).at(u, 2))
                wait(pool, ready["CT"], ctx_index(u))
                r = nrs[:, :].rearrange("p (t o) -> p t o", o=1).to_broadcast([P, QT + CT_N, D])
                nc.gpsimd.tensor_tensor(xn[:, :, :], xin[:, :, :], r[:, 0:QT, :], ALU.mult)
                nc.gpsimd.tensor_tensor(cn[:, :, :], cin[u.parity][:, :, :], r[:, QT:, :], ALU.mult
                                        ).then_inc(inputs_normed, 1)

            def split(u, src, rest, parts, n, have, steps):
                pool.wait_ge(have, ONE.whole(u))
                wait(pool, parts_stored, PerUnit(32).at(u, 0))
                alone(pool)
                nc.gpsimd.tensor_copy(parts[:, 0, 0:n], src[:, 0:n]).then_inc(steps, 1)
                pool.wait_ge(steps, FOUR.at(u, 1))
                nc.gpsimd.tensor_tensor(rest[:, 0:n], src[:, 0:n], parts[:, 0, 0:n], ALU.subtract).then_inc(steps, 1)
                pool.wait_ge(steps, FOUR.at(u, 2))
                alone(pool)
                nc.gpsimd.tensor_copy(parts[:, 1, 0:n], rest[:, 0:n]).then_inc(steps, 1)
                pool.wait_ge(steps, FOUR.at(u, 3))
                nc.gpsimd.tensor_tensor(parts[:, 2, 0:n], rest[:, 0:n], parts[:, 1, 0:n], ALU.subtract
                                        ).then_inc(steps, 1)

            def residual(u):
                wait(pool, taken["O"], ONE.at(u, 0))
                if u.stage < 2:
                    alone(pool)
                    ins = nc.gpsimd.tensor_tensor(xb[:, :, :], xs[:, u.batch, :, :], rows_of(bo2[u.stage][:, :], QT),
                                                  ALU.add)
                else:
                    alone(pool)
                    ins = nc.gpsimd.tensor_copy(xb[:, :, :], xs[:, u.batch, :, :])
                ins.then_inc(xb_ready, 1)

            def normalise(u):
                pool.wait_ge(taken["D"], ONE.whole(u))
                wait(pool, ready["O"], ONE.at(u, 0))
                nc.gpsimd.tensor_tensor(att[:, :], raw[:, :], rden[:, :], ALU.mult).then_inc(att_ready, 1)

            def root(u):
                if u.stage < 2:
                    pool.wait_ge(stats_ready, TWO.whole(u))
                    src = bag[:, 0:QT, 1:2].rearrange("p t o -> p (t o)")
                    alone(pool)
                    nc.gpsimd.tensor_scalar(yms[:, 0:QT], src, LN_EPS, None, ALU.add).then_inc(rs_steps, 1)
                else:
                    pool.wait_ge(norm_steps, TWO.whole(u))
                    alone(pool)
                    nc.gpsimd.tensor_scalar(yms[:, 0:QT], ysum[:, 0:QT], 1.0 / D, RMS_EPS, ALU.mult, ALU.add
                                            ).then_inc(rs_steps, 1)
                pool.wait_ge(rs_steps, TWO.at(u, 1))
                nc.gpsimd.tensor_tensor(yrs[:, 0:QT], yms[:, 0:QT], minushalf[:, 0:QT], ALU.pow
                                        ).then_inc(rs_steps, 1)

            def affine(u):
                pool.wait_ge(normed, TWO.whole(u))
                g = rows_of(gam[u.stage if u.stage < 2 else 3], QT)
                if u.stage < 2:
                    nc.gpsimd.tensor_tensor(zg[:, 0:QT, :], z[:, 0:QT, :], g, ALU.mult).then_inc(affine_steps, 1)
                    pool.wait_ge(affine_steps, ONE.whole(u))
                    alone(pool)
                    nc.gpsimd.tensor_tensor(xs[:, u.batch, :, :], zg[:, 0:QT, :], rows_of(bet[u.stage], QT),
                                            ALU.add).then_inc(x_ready, 1)
                else:
                    wait(pool, out_stored, u.batch * 16)
                    nc.gpsimd.tensor_tensor(zg[:, 0:QT, :], z[:, 0:QT, :], g, ALU.mult).then_inc(affine_steps, 1)

            def step(u, main):
                before, nxt, nxt2 = neighbours(u)
                if nxt2 is not None:
                    copy_input(nxt2)
                    if nxt2.stage == 2:
                        norm_inputs(nxt2)
                if before is not None:
                    residual(before)
                    normalise(before)
                if nxt2 is not None:
                    split(nxt2, qf, qr, qs, LQ, taken["Q"], q_steps)
                if u.stage == 0 and nxt2 is not None:
                    split(nxt2, kf, kr, ks, KEYS[nxt2.stage], taken["K"], k_steps)
                elif nxt2 is not None:
                    split(nxt2, kf, kr, ks, KEYS[nxt2.stage], taken["K"], k_steps)
                if before is not None:
                    root(before)
                    affine(before)

            def feed_forward():
                pool.wait_ge(x_ready, 2 * B)
                flat = xs[:, :, :, :].rearrange("p b t d -> p (b t) d")
                with pool.Fori(0, 4) as i:
                    pool.wait_ge(f_ready, i + 1)
                    alone(pool)
                    nc.gpsimd.tensor_copy(xf[:, :, :], flat[:, bass.ds(i * 4, 4), :]).then_inc(f_copied, 1)
                    pool.wait_ge(f_y, i + 1)
                    pool.wait_ge(f_copied, i + 1)
                    nc.gpsimd.tensor_tensor(xfb[:, :, :], xf[:, :, :], rows_of(b2b, 4), ALU.add).then_inc(f_xb, 1)
                    pool.wait_ge(f_stats, i * 8 + 8)
                    alone(pool)
                    nc.gpsimd.tensor_scalar(yms[:, 0:4], bag[:, :, 1:2].rearrange("p t o -> p (t o)"), LN_EPS, None,
                                            ALU.add).then_inc(f_rs, 1)
                    pool.wait_ge(f_rs, i * 2 + 1)
                    nc.gpsimd.tensor_tensor(yrs[:, 0:4], yms[:, 0:4], minushalf[:, 0:4], ALU.pow).then_inc(f_rs, 1)
                    pool.wait_ge(f_normed, i * 4 + 4)
                    nc.gpsimd.tensor_tensor(zg[:, :, :], z[:, :, :], rows_of(gam[2], 4), ALU.mult).then_inc(f_aff, 1)
                    pool.wait_ge(f_aff, i + 1)
                    alone(pool)
                    nc.gpsimd.tensor_tensor(flat[:, bass.ds(i * 4, 4), :], zg[:, :, :], rows_of(bet[2], 4), ALU.add
                                            ).then_inc(f_x, 1)

            schedule(pool, step, feed_forward)



def shape_constants():
    bf = np.dtype("bfloat16")
    c = {}
    c["c_ident"] = np.eye(P, dtype=np.float32)
    c["c_identb"] = np.eye(P, dtype=np.float32).astype(bf)
    j = np.arange(2 * BLK)[:, None]
    i = np.arange(BLK)[None, :]
    band = (j <= i + BLK) & (j > i)
    first = band & (j >= BLK)
    c["c_mask_t"] = np.where(np.concatenate([first] + [band] * (NBLK - 1), 1), 0.0, NEG).astype(bf)
    c["c_mask_q"] = np.where(np.stack([np.concatenate([first.T, band.T]), np.concatenate([band.T, band.T])], 1),
                             0.0, NEG).astype(bf)
    spread = np.zeros((P, P), np.float32)
    tiny = np.zeros((P, 1), np.float32)
    for p in range(P):
        spread[16 * (p // 16) + DH, p] = 1.0
        tiny[p] = TINY if p % 16 >= DH else 0.0
    c["c_spread"], c["c_dentiny"] = spread, tiny
    slope = 2.0 ** (-8.0 * np.arange(1, H + 1) / H)
    place = np.arange(PAD + LQ) - (PAD + LQ) // 2
    rest = (slope[:, None] * place[None, :] / SCALE)
    parts = []
    for _ in range(3):
        parts.append(rest.astype(bf))
        rest = rest - parts[-1].astype(np.float64)
    c["c_slopes"] = np.stack(parts)
    c["c_ones"] = np.ones((3, H, LQ), bf)
    c["c_zeros"] = np.zeros((3, H, LK), bf)
    return c


def head_rows(m):
    m = np.asarray(m).reshape(2, 2, 4, DH, -1).transpose(2, 1, 3, 0, 4)
    placed = np.zeros((4, 2, 2 * DH, 2, m.shape[-1]), m.dtype)
    placed[:, :, :DH] = m
    return placed.reshape(P, 2, m.shape[-1])


def kernel(**inputs):
    import concourse.bacc as _bacc
    from concourse import mybir as _mybir
    from concourse.bass_utils import run_bass_kernel_spmd as _run

    nc = _bacc.Bacc("TRN2", target_bir_lowering=False, num_devices=1)
    given = dict(inputs)

    def take(*names):
        return [np.asarray(given.pop(n)) for n in names]

    given["w_in"] = np.stack(take("L0_xattn_swq", "L0_xattn_swk", "L0_xattn_swv", "L0_xattn_cwq", "L0_xattn_cwk",
                                  "L0_xattn_cwv", "L1_xattn_Wq", "L1_xattn_Wk", "L1_xattn_Wv"), 1)
    given["w_out"] = np.stack([head_rows(m) for m in take("L0_xattn_swo", "L0_xattn_cwo", "L1_xattn_Wo")], 1)
    given["columns"] = np.concatenate(
        [v.reshape(-1, P).T for v in take("L0_xattn_sbq", "L0_xattn_sbk", "L0_xattn_cbq", "L0_xattn_cbk",
                                          "L1_xattn_g_q", "L1_xattn_g_c", "L0_xattn_b1")]
        + [head_rows(v)[:, :, 0] for v in take("L0_xattn_sbv", "L0_xattn_cbv")], 1)
    given["vectors"] = np.stack(take("L0_xattn_sbo", "L0_xattn_cbo", "L0_xattn_b2", "L0_xattn_g1", "L0_xattn_g2",
                                     "L0_xattn_g3", "L1_xattn_g_out", "L0_xattn_be1", "L0_xattn_be2",
                                     "L0_xattn_be3"))
    given.update(shape_constants())
    arrays, args = {}, {}
    for name, value in given.items():
        value = np.ascontiguousarray(value)
        arrays[f"in_{name}_dram"] = value
        args[name] = nc.dram_tensor(f"in_{name}_dram", value.shape, _mybir.dt.from_np(value.dtype),
                                    kind="ExternalInput").ap()
    out = nc.dram_tensor("out_0_dram", (B, LQ, D), F32, kind="ExternalOutput").ap()
    two_layer_kernel(nc, args, out)
    r = _run(nc, [arrays], core_ids=[0])
    return r.results[0]["out_0_dram"]
```

```python
from contextlib import ExitStack

import numpy as np

import concourse.bass as bass
from concourse import mybir

ALU = mybir.AluOpType
ACT = mybir.ActivationFunctionType
AX = mybir.AxisListType
F32 = mybir.dt.float32
BF16 = mybir.dt.bfloat16
U8 = mybir.dt.uint8

B, LQ, LK, D, H, FF, WIN = 8, 256, 512, 128, 16, 512, 64
DH = D // H
P = 128
QT = LQ // P
CT_N = LK // P
BLK = WIN
NBLK = LQ // BLK
PAD = BLK
SCALE = float(DH) ** -0.5
NEG = -1.0e30
CAP = 1.0e20
TINY = 1.0e-30
LN_EPS, RMS_EPS = 1e-5, 1e-6

PAIRS = (3, 2, 1)
NG = sum(PAIRS)
ROW_X = DH * NG
ROWS_MAX = 96
ROW_M = 96
ROWS_ALL = ROW_M + 3
QUADS = H // 4

KEYS = (LQ, LK, LK)
TILES = (QUADS, H, H)
MAXT = (QT * QUADS, QT * H, QT * H)

PV_LAG = 5


class Slot:

    def __init__(self, tile=None, share=(0, 0), values=(), raw=False, split=None, norm=False, hidden=False,
                 small=()):
        self.tile, self.share, self.values = tile, share, values
        self.raw, self.split, self.norm, self.hidden, self.small = raw, split, norm, hidden, small

    def maxima(self, u):
        n = MAXT[u.stage]
        return range(int(n * self.share[0]), int(n * self.share[1]))


def self_slots():
    quad = [[("own", q, c) for c in range(4)] for q in range(QUADS)]
    return [
        Slot(tile=0, split=1, raw=True, small=("M1",)),
        Slot(tile=1, small=("D",)),
        Slot(share=(0, 1 / 4), values=quad[0], small=("XT",)),
        Slot(share=(1 / 4, 2 / 4), small=("CT", "A", "Q")),
        Slot(tile=2, split=0, values=quad[1], small=("K",)),
        Slot(tile=3, share=(2 / 4, 3 / 4), small=("O", "M0")),
        Slot(share=(3 / 4, 1), values=quad[2]),
        Slot(norm=True, values=quad[3], small=("V",)),
    ]


def cross_slots(small, norm):
    rest = {0: (11, 12), 1: (13,), 2: (14,), 3: (15,)}
    slots = []
    for t in range(H):
        values = [("before", k // 4, k % 4) for k in rest.get(t, ())]
        if t >= PV_LAG:
            values += [("own", (t - PV_LAG) // 4, (t - PV_LAG) % 4)]
        slots.append(Slot(tile=t, share=(t / H, (t + 1) / H), values=values, raw=t == 4,
                          split={0: 1, 8: 0}.get(t), norm=t == norm, hidden=t == 12, small=small.get(t, ())))
    return slots


CROSS_1 = {1: ("M1",), 2: ("XT",), 3: ("CT",), 4: ("Q",), 5: ("D",), 6: ("K",), 7: ("A",), 8: ("O",), 9: ("M0",),
           11: ("X2",), 13: ("V",), 15: ("F",)}
CROSS_2 = {1: ("M1",), 3: ("XT",), 4: ("CT",), 5: ("D",), 6: ("Q",), 7: ("A",), 8: ("K",), 9: ("O",), 10: ("M0",),
           13: ("V",)}
SLOTS = (self_slots(), cross_slots(CROSS_1, 9), cross_slots(CROSS_2, 11))


class Unit:

    def __init__(self, stage, batch, parity):
        self.stage, self.batch, self.parity = stage, batch, parity

    def shift(self, d):
        if not isinstance(self.batch, int):
            return Unit(self.stage, self.batch + d, (self.parity + d) % 2)
        s, b = divmod(self.stage * B + self.batch + d, B)
        return Unit(s, b, b % 2) if 0 <= s < 3 else None


class PerUnit:

    def __init__(self, n0, n1=None, n2=None):
        self.n = (n0, n0 if n1 is None else n1, n0 if n2 is None else n2, 0)

    def at(self, u, k):
        return sum(self.n[:u.stage]) * B + u.batch * self.n[u.stage] + k

    def whole(self, u):
        return self.at(u, self.n[u.stage])


ONE = PerUnit(1)
TWO = PerUnit(2)
SCORES = PerUnit(*TILES)
MAXIMA = PerUnit(*MAXT)
QUAD4 = PerUnit(QUADS)
THREE = PerUnit(3)
FIVE = PerUnit(5)
STACKS = PerUnit(32, 32, 48)
DMA1 = PerUnit(16)
STORES = PerUnit(16 * 6)
FFN = PerUnit(0, 1, 0)
FFN2 = PerUnit(0, 2, 0)
LAYER1 = PerUnit(0, 0, 1)


def schedule(eng, step):
    step(Unit(0, -2, 0))
    step(Unit(0, -1, 1))
    for stage in range(3):
        step(Unit(stage, 0, 0))
        with eng.Fori(0, 2) as i:
            step(Unit(stage, i * 2 + 1, 1))
            step(Unit(stage, i * 2 + 2, 0))
        for b in (5, 6, 7):
            step(Unit(stage, b, b % 2))
    step(Unit(3, 0, 0))


def in_flight(u):
    main = not isinstance(u.batch, int) or (u.batch >= 0 and u.stage < 3)
    return main, u.shift(-1), u.shift(1), u.shift(2)


def slots_of(u):
    if u.stage == 2 and isinstance(u.batch, int) and u.batch == 0:
        return SLOTS[1]
    return SLOTS[min(u.stage, 2)]


def wait(eng, sem, value):
    if not isinstance(value, int) or value > 0:
        eng.wait_ge(sem, value)


def two_layer_kernel(nc, a, out):
    with ExitStack() as ctx:
        def sb(name, shape, dt=F32):
            return ctx.enter_context(nc.sbuf_tensor(name, shape, dt))

        def sem(name):
            return ctx.enter_context(nc.semaphore(name))

        st = ctx.enter_context(nc.psum_tensor("st", [P, 2, 1024], F32))
        mx = ctx.enter_context(nc.psum_tensor("mx", [P, 2, 512], F32))
        pv = ctx.enter_context(nc.psum_tensor("pv", [P, 512], F32))
        misc = ctx.enter_context(nc.psum_tensor("misc", [P, 512], F32))
        misc_bf = misc[:, :].bitcast(BF16)

        kst = [sb(f"kst{i}", [P, H, LK], BF16) for i in range(2)]
        qst = [sb(f"qst{i}", [P, H, LQ], BF16) for i in range(2)]
        probs = sb("probs", [P, QUADS, 4 * 1024])
        vp = [sb(f"vp{i}", [P, 4, H, 32]) for i in range(2)]
        xs = sb("xs", [P, B, QT, D])
        xin, xn = sb("xin", [P, QT, D]), sb("xn", [P, QT, D])
        cin = [sb(f"cin{i}", [P, CT_N, D]) for i in range(2)]
        cn = sb("cn", [P, CT_N, D])
        xT = [sb(f"xT{i}", [P, PAD + LQ]) for i in range(2)]
        cT = [sb(f"cT{i}", [P, LK]) for i in range(2)]
        qf, kf = sb("qf", [P, LQ]), sb("kf", [P, LK])
        qr, kr = sb("qr", [P, LQ]), sb("kr", [P, LK])
        qs, ks = sb("qs", [P, 3, LQ], BF16), sb("ks", [P, 3, LK], BF16)
        negmax = sb("negmax", [P, QT, H])
        mcap = [sb(f"mcap{i}", [P, QT, H // 2]) for i in range(2)]
        mrest = [sb(f"mrest{i}", [P, QT, H // 2]) for i in range(2)]
        msplit = [sb(f"msplit{i}", [P, QT, P], BF16) for i in range(2)]
        mT = [sb(f"mT{i}", [3 * H // 2, LQ], BF16) for i in range(2)]
        raw = sb("raw", [P, 512])
        den, rden = sb("den", [P, 4, 8]), sb("rden", [P, 4, 8])
        att = sb("att", [P, QT, D])
        attT = sb("attT", [P, LQ])
        xb = sb("xb", [P, QT, D])
        nsq, nsum, nms, nrs = sb("nsq", [P, D]), sb("nsum", [P, 6]), sb("nms", [P, 6]), sb("nrs", [P, 6])
        minushalf = sb("minushalf", [P, 8])
        x2, x2b = sb("x2", [P, QT, D]), sb("x2b", [P, QT, D])
        x2T = sb("x2T", [P, LQ])
        hT = sb("hT", [P, FF // P, LQ])

        class Norm:

            def __init__(self, name, per):
                self.y, self.z, self.zg = (sb(name + n, [P, QT, D]) for n in ("_y", "_z", "_zg"))
                self.bst, self.bag = sb(name + "_bst", [P, QT, 6]), sb(name + "_bag", [P, QT, 2])
                self.sq, self.ysum = sb(name + "_sq", [P, D]), sb(name + "_ysum", [P, QT])
                self.ms, self.rs = sb(name + "_ms", [P, QT]), sb(name + "_rs", [P, QT])
                self.stats, self.root = sem(name + "_stats"), sem(name + "_root")
                self.normed, self.scaled = sem(name + "_normed"), sem(name + "_scaled")
                self.n_stats, self.two, self.one = per

        attn_norm = Norm("attn", (PerUnit(4, 4, 2), TWO, ONE))
        ffn_norm = Norm("ffn", (PerUnit(0, 4, 0), FFN2, FFN))

        ident = sb("ident", [P, P])
        identb = sb("identb", [P, P], BF16)
        mask_t = sb("mask_t", [P, LQ], BF16)
        mask_q = sb("mask_q", [P, QT, P], BF16)
        pick = sb("pick", [P, 72])
        win = sb("win", [P, 9, P])
        w = {n + str(s): win[:, 3 * s + i, :] for s in range(2) for i, n in enumerate("qkv")}
        w.update({n + "2": sb("w2" + n, [P, P])[:, :] for n in "qkv"})
        wo = sb("wo", [P, 3, D])
        w1, w2 = sb("w1", [P, FF]), sb("w2", [P, FF // P, D])
        cols = sb("cols", [P, 12])
        bvb = sb("bvb", [P, 2, P])
        zero = sb("zero", [P, P])
        bo2 = [sb(f"bo2{s}", [P, D]) for s in range(2)]
        rows = sb("rows", [P, 10, D])
        bob = [rows[:, s, :] for s in range(2)]
        b2b = rows[:, 2, :]
        gam = [rows[:, 3 + i, :] for i in range(4)]
        bet = [rows[:, 7 + i, :] for i in range(3)]
        kmu = sb("kmu", [B, LK], U8)
        kmask = sb("kmask", [B, LK], BF16)

        qd = nc.dram_tensor("q_parts", [P, NG, LQ], BF16).ap()
        kd = nc.dram_tensor("k_parts", [P, NG, LK], BF16).ap()
        kmd = nc.dram_tensor("key_mask_rows", [B, LK], BF16).ap()
        qd_rows = qd.rearrange("(h d) g q -> (d g) h q", d=DH)
        kd_rows = kd.rearrange("(h d) g q -> (d g) h q", d=DH)

        consts_loaded = sem("consts_loaded")
        x_loaded = sem("x_loaded")
        stack_consts = sem("stack_consts")
        mask_loaded, mask_made, mask_stored = sem("mask_loaded"), sem("mask_made"), sem("mask_stored")
        dve_set, pool_set = sem("dve_set"), sem("pool_set")
        weights_made = sem("weights_made")
        bias_product = sem("bias_product")
        bias_made = sem("bias_made")
        ctx_loaded = [sem("ctx_loaded0"), sem("ctx_loaded1")]
        x_copied = sem("x_copied")
        squares_summed = sem("squares_summed")
        means_made = sem("means_made")
        inputs_normed = sem("inputs_normed")
        names = ("V", "XT", "CT", "D", "Q", "K", "A", "O", "M0", "M1", "X2", "F")
        ready = {n: sem("ready_" + n) for n in names}
        taken = {n: sem("taken_" + n) for n in names}
        q_steps, k_steps = sem("q_steps"), sem("k_steps")
        parts_stored = sem("parts_stored")
        stacks_loaded = [sem("stacks_loaded0"), sem("stacks_loaded1")]
        zeros_loaded = [[sem(f"zeros_loaded{i}_{half}") for half in range(2)]
                        for i in range(2)]
        m_steps = [sem("m_steps0"), sem("m_steps1")]
        mrows_loaded = [sem("mrows_loaded0"), sem("mrows_loaded1")]
        scores_ready, exp_done = sem("scores_ready"), sem("exp_done")
        pv_done = sem("pv_done")
        maxin_ready, max_done = sem("maxin_ready"), sem("max_done")
        raw_ready = sem("raw_ready")
        den_steps = sem("den_steps")
        xb_ready = sem("xb_ready")
        x_ready = sem("x_ready")
        x2_steps = sem("x2_steps")
        hidden_ready, gelu_done = sem("hidden_ready"), sem("gelu_done")
        out_stored = sem("out_stored")
        waits_passed = sem("waits_passed")

        COUNT = {n: ONE for n in names}
        COUNT["CT"] = PerUnit(0, 1, 1)
        COUNT["X2"] = COUNT["F"] = FFN
        CREDIT = {n: int(n == "F") for n in names}
        DVE_SETS, POOL_SETS = 10, 6
        CTX_LOADS = PerUnit(0, 8, 8)
        SQUARES = PerUnit(0, 0, QT + CT_N)
        HALVES = ((0, H // 2), (H // 2, H))

        def alone(eng):
            eng.sem_inc(waits_passed, 1)

        def ctx_value(u):
            if isinstance(u.batch, int):
                return CTX_LOADS.at(u, 0) - 8 * u.parity + 16
            return CTX_LOADS.at(u, 16 - 8 * u.parity)

        def has(name, u):
            if u is None or (name == "CT" and u.stage == 0):
                return False
            return name not in ("X2", "F") or u.stage == 1

        def units(u, before, nxt, nxt2):
            return {"V": nxt, "M0": nxt, "M1": u if in_flight(u)[0] else None, "XT": nxt2, "CT": nxt2, "Q": nxt2, "K": nxt2,
                    "D": before, "A": before, "O": before, "X2": before, "F": before}

        block = ctx.enter_context(nc.Block())

        def const_loads():
            yield ident[:, :], a["c_ident"]
            yield win[:, :, :], a["w_in"]
            yield cols[:, :], a["columns"]
            yield wo[:, :, :], a["w_out"]
            yield identb[:, :], a["c_identb"]
            yield mask_t[:, :], a["c_mask_t"]
            yield mask_q[:, :, :], a["c_mask_q"]
            yield pick[:, :], a["c_pick"]
            yield rows[:, :, :], a["vectors"].rearrange("(o v) d -> o v d", o=1).to_broadcast([P, 10, D])
            yield w1[:, :], a["L0_xattn_w1"]
            yield w2[:, :, :], a["L0_xattn_w2"].rearrange("(f p) d -> p f d", p=P)

        CONSTS = 16 * len(list(const_loads()))

        @block.sync
        def _(sp):
            sp.dma_start(xs[:, :, :, :], a["x"].rearrange("b (t p) d -> p b t d", p=P)).then_inc(x_loaded, 16)
            for dst, src in const_loads():
                sp.dma_start(dst, src).then_inc(consts_loaded, 16)
            sp.dma_start(kmu[:, :], a["mask_BxS2_bf1"]).then_inc(mask_loaded, 16)
            sp.wait_ge(pool_set, POOL_SETS)
            sp.wait_ge(dve_set, DVE_SETS)
            for i in range(2):
                sp.dma_start(qst[i][ROW_X:ROW_X + 3, :, :], a["c_ones"]).then_inc(stack_consts, 16)
                sp.dma_start(kst[i][ROW_X:ROW_X + 3, :, 0:PAD + LQ], a["c_slopes"]).then_inc(stack_consts, 16)
            sp.wait_ge(mask_made, 1)
            sp.dma_start(kmd, kmask[:, :]).then_inc(mask_stored, 16)
            sp.wait_ge(mask_stored, 16)

            def load_context(u):
                if u is None or u.stage == 0:
                    return
                wait(sp, ready["CT"], COUNT["CT"].at(u, -1))
                wait(sp, inputs_normed, LAYER1.at(u, -1)) if u.stage == 2 else None
                sp.dma_start(cin[u.parity][:, :, :],
                             a["ctx_1024"][u.batch].rearrange("(t p) d -> p t d", p=P)
                             ).then_inc(ctx_loaded[u.parity], 16)

            def load_stacks(n, half):
                loaded = stacks_loaded[half]
                heads = slice(*HALVES[half])
                nk = KEYS[n.stage]
                col = PAD if n.stage == 0 else 0
                sp.dma_start(qst[n.parity][0:ROW_X, heads, :], qd_rows[:, heads, :]).then_inc(loaded, 16)
                sp.dma_start(kst[n.parity][0:ROW_X, heads, col:col + nk], kd_rows[:, heads, 0:nk]
                             ).then_inc(loaded, 16)
                extra = kst[n.parity][ROW_X:ROW_X + 3, heads, :]
                if n.stage == 1 and isinstance(n.batch, int) and n.batch < 2:
                    sp.dma_start(extra, a["c_zeros"]).then_inc(zeros_loaded[n.parity][half], 16)
                elif n.stage == 2:
                    src = kmd[n.batch].rearrange("(o p k) -> o p k", o=1, p=1)
                    sp.dma_start(extra[0:1, :, :], src.to_broadcast([1, H // 2, LK])).then_inc(loaded, 16)

            def load_maxima(u, half):
                sp.wait_ge(taken[f"M{half}"], ONE.whole(u))
                sp.dma_start(qst[u.parity][ROW_M:ROW_M + 3, slice(*HALVES[half]), :], mT[half][:, :]
                             ).then_inc(mrows_loaded[half], 16)

            def step(u):
                main, before, nxt, n = in_flight(u)
                if main:
                    load_maxima(u, 1)
                if n is not None:
                    nk = KEYS[n.stage]
                    for half in range(2):
                        wait(sp, stacks_loaded[half], STACKS.at(n, 0))
                    q_dst, k_dst = 0, 0
                    sp.wait_ge(q_steps, THREE.whole(n))
                    for count in PAIRS:
                        sp.dma_start(qd[:, q_dst:q_dst + count, :], qs[:, 0:count, :]).then_inc(parts_stored, 16)
                        q_dst += count
                    sp.wait_ge(k_steps, THREE.whole(n))
                    for part, count in enumerate(PAIRS):
                        sp.dma_start(kd[:, k_dst:k_dst + count, 0:nk],
                                     ks[:, part:part + 1, 0:nk].to_broadcast([P, count, nk])
                                     ).then_inc(parts_stored, 16)
                        k_dst += count
                    sp.wait_ge(parts_stored, STORES.whole(n))
                    if main:
                        sp.wait_ge(scores_ready, SCORES.at(u, TILES[u.stage] // 2))
                    load_stacks(n, 0)
                    if u.stage == 0:
                        if main:
                            sp.wait_ge(scores_ready, SCORES.whole(u))
                        load_stacks(n, 1)
                load_context(n.shift(1) if n is not None else None)
                if nxt is not None:
                    load_maxima(nxt, 0)
                if n is not None and u.stage > 0:
                    sp.wait_ge(scores_ready, SCORES.whole(u))
                    load_stacks(n, 1)
                if before is not None and before.stage == 2:
                    sp.wait_ge(attn_norm.scaled, ONE.whole(before))
                    sp.dma_start(out[before.batch].rearrange("(t p) d -> p t d", p=P),
                                 attn_norm.zg[:, :, :]).then_inc(out_stored, 16)

            schedule(sp, step)
            sp.wait_ge(out_stored, 16 * B)

        @block.tensor
        def _(pe):
            pe.wait_ge(consts_loaded, CONSTS)
            pe.wait_ge(weights_made, 3)
            pe.wait_ge(bias_made, 2)
            for s in range(2):
                mm = nc.tensor.matmul(misc[:, s * D:(s + 1) * D], bvb[:, s, :], wo[:, s, :], start=True, stop=True)
            mm.then_inc(bias_product, 1)
            pe.wait_ge(bias_made, 4)

            def scores(u, t):
                if t % (TILES[u.stage] // 2) == 0:
                    pe.wait_ge(mrows_loaded[t // (TILES[u.stage] // 2)], DMA1.whole(u))
                wait(pe, exp_done, SCORES.at(u, t - 1))
                dst = st[:, t % 2, :]
                k, q = kst[u.parity], qst[u.parity]
                if u.stage == 0:
                    for half in range(2):
                        nc.tensor.matmul(dst[:, 512 * half:512 * half + 512].rearrange("p (h q) -> p h q", h=2),
                                         identb[:, :],
                                         mask_t[:, :].rearrange("p (o q) -> p o q", o=1).to_broadcast([P, 2, LQ]),
                                         start=True, stop=False, skip_group_check=True)
                        for j in (2 * half, 2 * half + 1):
                            for c in range(NBLK):
                                at = j * LQ + c * BLK
                                mm = nc.tensor.matmul(
                                    dst[:, at:at + BLK],
                                    k[0:ROWS_ALL, 4 * t + j, c * BLK:c * BLK + 2 * BLK],
                                    q[0:ROWS_ALL, 4 * t + j, c * BLK:(c + 1) * BLK],
                                    start=False, stop=(c == NBLK - 1), skip_group_check=True)
                else:
                    for c in range(CT_N):
                        mm = nc.tensor.matmul(dst[:, c * LQ:(c + 1) * LQ],
                                              k[0:ROWS_ALL, t, c * P:(c + 1) * P],
                                              q[0:ROWS_ALL, t, :], start=True, stop=True)
                mm.then_inc(scores_ready, 1)

            def max_scores(u, n):
                for half in range(2):
                    if n == half * MAXT[u.stage] // 2:
                        pe.wait_ge(stacks_loaded[half], STACKS.whole(u))
                        if u.stage == 1 and isinstance(u.batch, int) and u.batch < 2:
                            pe.wait_ge(zeros_loaded[u.parity][half], 16)
                wait(pe, max_done, MAXIMA.at(u, n - 1))
                dst = mx[:, n % 2, :]
                k, q = kst[u.parity], qst[u.parity]
                if u.stage == 0:
                    tile, quad = n % QT, n // QT
                    nc.tensor.matmul(dst.rearrange("p (h k) -> p h k", h=4), identb[:, :],
                                     mask_q[:, tile:tile + 1, :].to_broadcast([P, 4, P]),
                                     start=True, stop=False, skip_group_check=True)
                    for j in range(4):
                        for half in range(2):
                            c = 2 * tile + half
                            mm = nc.tensor.matmul(
                                dst[BLK * half:BLK * half + BLK, j * P:(j + 1) * P],
                                q[0:ROWS_MAX, 4 * quad + j, c * BLK:(c + 1) * BLK],
                                k[0:ROWS_MAX, 4 * quad + j, c * BLK:c * BLK + 2 * BLK],
                                start=False, stop=(j == 3), skip_group_check=True)
                else:
                    tile, head = n % QT, n // QT
                    mm = nc.tensor.matmul(dst, q[0:ROWS_MAX, head, tile * P:(tile + 1) * P],
                                          k[0:ROWS_MAX, head, :], start=True, stop=True)
                mm.then_inc(maxin_ready, 1)

            def weighted_values(u, quad, c):
                if c == 0:
                    last = quad + 1 if u.stage == 0 else 4 * quad + 4
                    pe.wait_ge(exp_done, SCORES.at(u, last))
                    if quad == 0:
                        pe.wait_ge(taken["V"], ONE.whole(u))
                        wait(pe, raw_ready, ONE.at(u, 0))
                region = quad // 2
                n = BLK if u.stage == 0 else LQ
                for j in range(4):
                    src = j * 4 * n + c * n
                    dst = region * LQ + (c * BLK if u.stage == 0 else 0)
                    mm = nc.tensor.matmul(pv[32 * j:32 * j + 32, dst:dst + n], vp[u.parity][:, c, 4 * quad + j, :],
                                          probs[:, quad, src:src + n], start=(quad == 0 and c == 0),
                                          stop=(quad == QUADS - 1 and c == 3), skip_group_check=True)
                if c == 3:
                    mm.then_inc(pv_done, 1)

            def hidden(u):
                pe.wait_ge(taken["X2"], FFN.whole(u))
                for f in range(FF // P):
                    mm = nc.tensor.matmul(st[:, 1, f * LQ:(f + 1) * LQ], w1[:, f * P:(f + 1) * P], x2T[:, :],
                                          start=True, stop=True)
                mm.then_inc(hidden_ready, 1)

            def small(name, u):
                s = u.stage
                if name == "V":
                    for c in range(4):
                        x, ct = xT[u.parity], cT[u.parity]
                        src = x[:, c * BLK:c * BLK + P] if s == 0 else ct[:, c * P:(c + 1) * P]
                        mm = nc.tensor.matmul(misc[:, c * P:(c + 1) * P], src, w[f"v{s}"], start=True, stop=True)
                elif name == "XT":
                    if s == 2:
                        pe.wait_ge(inputs_normed, LAYER1.whole(u))
                    else:
                        pe.wait_ge(x_copied, ONE.whole(u))
                    src = xn if s == 2 else xin
                    for t in range(QT):
                        mm = nc.tensor.transpose(misc[:, t * P:(t + 1) * P], src[:, t, :], ident[:, :])
                elif name == "CT":
                    if s == 1:
                        pe.wait_ge(ctx_loaded[u.parity], ctx_value(u))
                    src = cn if s == 2 else cin[u.parity]
                    for t in range(CT_N):
                        mm = nc.tensor.transpose(misc[:, t * P:(t + 1) * P], src[:, t, :], ident[:, :])
                elif name == "Q":
                    pe.wait_ge(taken["XT"], ONE.whole(u))
                    mm = nc.tensor.matmul(misc[:, 0:LQ], w[f"q{s}"], xT[u.parity][:, PAD:PAD + LQ],
                                          start=True, stop=True)
                elif name == "K":
                    src = xT[u.parity][:, PAD:PAD + LQ] if s == 0 else cT[u.parity][:, :]
                    if s > 0:
                        pe.wait_ge(taken["CT"], COUNT["CT"].whole(u))
                    mm = nc.tensor.matmul(misc[:, 0:KEYS[s]], w[f"k{s}"], src, start=True, stop=True)
                elif name == "D":
                    pe.wait_ge(raw_ready, ONE.whole(u))
                    for t in range(QT):
                        for r in range(2):
                            at = (2 * t + r) * 72
                            mm = nc.tensor.matmul(misc[:, at:at + 72], raw[:, r * LQ + t * P:r * LQ + (t + 1) * P],
                                                  pick[:, :], start=True, stop=True)
                elif name == "A":
                    pe.wait_ge(taken["D"], ONE.whole(u))
                    for t in range(QT):
                        mm = nc.tensor.transpose(misc[:, t * P:(t + 1) * P], att[:, t, :], ident[:, :])
                elif name == "O":
                    pe.wait_ge(taken["A"], ONE.whole(u))
                    for t in range(QT):
                        mm = nc.tensor.matmul(misc[:, t * D:(t + 1) * D], attT[:, t * P:(t + 1) * P], wo[:, s, :],
                                              start=True, stop=True)
                elif name in ("M0", "M1"):
                    half = int(name[1])
                    pe.wait_ge(m_steps[half], FIVE.whole(u))
                    for t in range(QT):
                        mm = nc.tensor.transpose(misc_bf[:, t * P:(t + 1) * P], msplit[half][:, t, :], identb[:, :])
                elif name == "X2":
                    pe.wait_ge(x2_steps, FFN2.at(u, 1))
                    for t in range(QT):
                        mm = nc.tensor.transpose(misc[:, t * P:(t + 1) * P], x2[:, t, :], ident[:, :])
                elif name == "F":
                    pe.wait_ge(gelu_done, FFN.whole(u))
                    for t in range(QT):
                        for f in range(FF // P):
                            mm = nc.tensor.matmul(misc[:, t * D:(t + 1) * D], hT[:, f, t * P:(t + 1) * P],
                                                  w2[:, f, :], start=(f == 0), stop=(f == FF // P - 1))
                mm.then_inc(ready[name], 1)

            def bank_free(u):
                static = isinstance(u.batch, int)
                if static and u.batch == -1:
                    pe.wait_ge(taken["K"], 1)
                if in_flight(u)[0]:
                    pe.wait_ge(taken["M0"], ONE.whole(u))
                    pe.wait_ge(taken["V"], ONE.whole(u))
                if u.stage == 1 and not (static and u.batch < 1):
                    pe.wait_ge(taken["F"], FFN.at(u, 0))
                elif u.stage == 2:
                    pe.wait_ge(taken["F"], B if static and u.batch == 0 else B + 1)
                elif u.stage == 3:
                    pe.wait_ge(taken["O"], ONE.at(u, -1))

            def step(u):
                main, before, nxt, n = in_flight(u)
                unit_of = units(u, before, nxt, n)
                last = None
                for slot in slots_of(u):
                    if slot.tile is not None and main:
                        if slot.tile == 13 and before is not None and before.stage == 1:
                            pe.wait_ge(gelu_done, FFN.whole(before))
                        scores(u, slot.tile)
                    todo = list(slot.maxima(nxt)) if nxt is not None else []
                    for k in todo[:1]:
                        max_scores(nxt, k)
                    for whose, quad, c in slot.values:
                        if whose == "own" and main:
                            weighted_values(u, quad, c)
                        elif whose == "before" and before is not None and before.stage > 0:
                            weighted_values(before, quad, c)
                    for k in todo[1:]:
                        max_scores(nxt, k)
                    if slot.hidden and before is not None and before.stage == 1:
                        pe.wait_ge(exp_done, SCORES.at(u, 12))
                        hidden(before)
                    for name in slot.small:
                        v = unit_of[name]
                        if not has(name, v):
                            continue
                        if last is None:
                            bank_free(u)
                        else:
                            pe.wait_ge(taken[last[0]], COUNT[last[0]].whole(last[1]) + CREDIT[last[0]])
                        small(name, v)
                        last = (name, v)

            pe.wait_ge(dve_set, DVE_SETS)
            pe.wait_ge(pool_set, POOL_SETS)
            pe.wait_ge(stack_consts, 64)
            schedule(pe, step)

        @block.scalar
        def _(act):
            act.wait_ge(consts_loaded, CONSTS)
            act.wait_ge(dve_set, DVE_SETS)
            act.wait_ge(pool_set, POOL_SETS)

            def take(name, u):
                s = u.stage
                if name == "V":
                    act.wait_ge(ready["V"], ONE.whole(u))
                    wait(act, pv_done, QUAD4.at(u, -QUADS))
                    for gg in range(2):
                        for r in range(2):
                            heads = slice(4 * (2 * r + gg), 4 * (2 * r + gg) + 4)
                            ins = nc.scalar.copy(
                                vp[u.parity][:, :, heads, 16 * gg:16 * gg + DH],
                                misc[:, :].rearrange("p (c h d) -> p c h d", c=4, h=H)[:, :, heads, :])
                    ins.then_inc(taken["V"], 1)
                elif name == "CT":
                    act.wait_ge(ready["CT"], COUNT["CT"].whole(u))
                    nc.scalar.copy(cT[u.parity][:, :], misc[:, :]).then_inc(taken["CT"], 1)
                elif name in ("Q", "K"):
                    n = LQ if name == "Q" else KEYS[s]
                    dst, parts, steps = (qf, qs, q_steps) if name == "Q" else (kf, ks, k_steps)
                    act.wait_ge(ready[name], ONE.whole(u))
                    wait(act, steps, THREE.at(u, 0))
                    wait(act, parts_stored, STORES.at(u, 0))
                    for k, to in enumerate((dst[:, 0:n], parts[:, 0, 0:n])):
                        if s == 2:
                            ins = nc.scalar.copy(to, misc[:, 0:n])
                        else:
                            col = 2 * s + (name == "K")
                            ins = nc.scalar.activation(to, misc[:, 0:n], ACT.Identity, bias=cols[:, col:col + 1])
                    ins.then_inc(taken[name], 1)
                elif name == "A":
                    act.wait_ge(ready["A"], ONE.whole(u))
                    wait(act, ready["O"], ONE.at(u, 0))
                    nc.scalar.copy(attT[:, :], misc[:, 0:LQ]).then_inc(taken["A"], 1)

            def square_inputs(u):
                act.wait_ge(x_copied, ONE.whole(u))
                act.wait_ge(ctx_loaded[u.parity], ctx_value(u))
                wait(act, means_made, PerUnit(0, 0, 2).at(u, 0))
                for t in range(QT + CT_N):
                    src = xin[:, t, :] if t < QT else cin[u.parity][:, t - QT, :]
                    wait(act, squares_summed, SQUARES.at(u, t))
                    nc.scalar.activation(nsq[:, :], src, ACT.Square, accum_out=nsum[:, t:t + 1]
                                         ).then_inc(squares_summed, 1)

            def step(u):
                main, before, nxt, n = in_flight(u)
                unit_of = units(u, before, nxt, n)
                for slot in slots_of(u):
                    if slot.tile is not None and main:
                        t = slot.tile
                        act.wait_ge(scores_ready, SCORES.at(u, t + 1))
                        quad, j = (t, 0) if u.stage == 0 else (t // 4, t % 4)
                        if j == 0:
                            wait(act, pv_done, QUAD4.at(u, quad + 1 - QUADS))
                        nc.scalar.activation(probs[:, quad, j * 1024:(j + 1) * 1024], st[:, t % 2, :],
                                             ACT.Exp, scale=SCALE).then_inc(exp_done, 1)
                    if slot.tile == 0 and n is not None and n.stage == 2:
                        square_inputs(n)
                    if slot.hidden and before is not None and before.stage == 1:
                        act.wait_ge(hidden_ready, FFN.whole(before))
                        act.wait_ge(taken["F"], FFN.at(before, 0) + CREDIT["F"])
                        for f in range(FF // P):
                            ins = nc.scalar.activation(hT[:, f, :], st[:, 1, f * LQ:(f + 1) * LQ], ACT.Gelu,
                                                       bias=cols[:, 6 + f:7 + f])
                        ins.then_inc(gelu_done, 1)
                    for name in slot.small:
                        if has(name, unit_of[name]):
                            take(name, unit_of[name])

            schedule(act, step)

        @block.vector
        def _(dve):
            nc.vector.memset(zero[:, :], 0.0).then_inc(dve_set, 1)
            dve.wait_ge(consts_loaded, CONSTS)
            dve.wait_ge(dve_set, 1)
            for i, (n, col) in enumerate((("q2", 4), ("k2", 5), ("v2", 5))):
                nc.vector.tensor_scalar(w[n], win[:, 6 + i, :], cols[:, col:col + 1], None, ALU.mult
                                        ).then_inc(weights_made, 1)
            for s in range(2):
                nc.vector.tensor_scalar(bvb[:, s, :], zero[:, :], cols[:, 10 + s:11 + s], None, ALU.add
                                        ).then_inc(bias_made, 1)
            for i in range(2):
                nc.vector.memset(xT[i][:, 0:PAD], 0.0).then_inc(dve_set, 1)
            nc.vector.memset(minushalf[:, :], -0.5).then_inc(dve_set, 1)
            dve.wait_ge(mask_loaded, 16)
            nc.vector.tensor_scalar(kmask[:, :], kmu[:, :], -NEG, NEG, ALU.mult, ALU.add).then_inc(mask_made, 1)
            dve.wait_ge(bias_product, 1)
            for s in range(2):
                nc.vector.tensor_tensor(bo2[s][:, :], misc[:, s * D:(s + 1) * D], bob[s], ALU.add
                                        ).then_inc(bias_made, 1)
            for i in range(2):
                nc.vector.memset(kst[i][0:ROWS_MAX, :, :].bitcast(mybir.dt.uint32), 0).then_inc(dve_set, 1)
                nc.vector.memset(kst[i][ROW_M:ROWS_ALL, :, :], 1.0).then_inc(dve_set, 1)
            dve.wait_ge(dve_set, 8)
            dve.wait_ge(pool_set, POOL_SETS)
            for i in range(2):
                for gg in range(2):
                    for r in range(2):
                        heads = slice(4 * (2 * r + gg), 4 * (2 * r + gg) + 4)
                        ins = nc.vector.memset(vp[i][:, :, heads, 16 * gg + DH:16 * gg + 2 * DH], 1.0)
                ins.then_inc(dve_set, 1)
            dve.sem_inc(taken["F"], 1)

            def maximum(u, n):
                dve.wait_ge(maxin_ready, MAXIMA.at(u, n + 1))
                if n % (MAXT[u.stage] // 2) == 0:
                    wait(dve, m_steps[n // (MAXT[u.stage] // 2)], FIVE.at(u, 0))
                tile = n % QT
                if u.stage == 0:
                    quad = n // QT
                    ins = nc.vector.tensor_reduce(negmax[:, tile, 4 * quad:4 * quad + 4],
                                                  mx[:, n % 2, :].rearrange("p (h k) -> p h k", h=4),
                                                  AX.X, ALU.max, negate=True)
                else:
                    ins = nc.vector.tensor_reduce(negmax[:, tile, n // QT:n // QT + 1], mx[:, n % 2, :],
                                                  AX.X, ALU.max, negate=True)
                ins.then_inc(max_done, 1)

            def split_maxima(u, half):
                steps, cap, rest = m_steps[half], mcap[half][:, :, :], mrest[half][:, :, :]
                dve.wait_ge(max_done, MAXIMA.at(u, MAXT[u.stage] * (half + 1) // 2))
                wait(dve, ready[f"M{half}"], ONE.at(u, 0))
                src = negmax[:, :, slice(*HALVES[half])]
                part = [msplit[half][:, :, i * H // 2:(i + 1) * H // 2] for i in range(3)]
                nc.vector.tensor_scalar(cap, src, CAP, None, ALU.min).then_inc(steps, 1)
                nc.vector.tensor_scalar(part[0], src, CAP, None, ALU.min).then_inc(steps, 1)
                dve.wait_ge(steps, FIVE.at(u, 2))
                nc.vector.tensor_tensor(rest, cap, part[0], ALU.subtract).then_inc(steps, 1)
                nc.vector.tensor_tensor(part[1], cap, part[0], ALU.subtract).then_inc(steps, 1)
                dve.wait_ge(steps, FIVE.at(u, 4))
                nc.vector.tensor_tensor(part[2], rest, part[1], ALU.subtract).then_inc(steps, 1)

            def take_raw(u):
                dve.wait_ge(pv_done, QUAD4.whole(u))
                wait(dve, ready["D"], ONE.at(u, 0))
                nc.vector.tensor_copy(raw[:, :], pv[:, :]).then_inc(raw_ready, 1)

            def statistics(chain, u, got, other, other_ready, square):
                name = got
                dve.wait_ge(ready[name], COUNT[name].whole(u))
                dve.wait_ge(*other_ready)
                nc.vector.tensor_tensor(chain.y[:, :, :].rearrange("p t d -> p (t d)"), misc[:, 0:QT * D],
                                        other[:, :, :].rearrange("p t d -> p (t d)"), ALU.add
                                        ).then_inc(taken[name], 1)
                dve.wait_ge(taken[name], COUNT[name].whole(u) + CREDIT[name])
                if not square:
                    for t in range(QT):
                        nc.vector.bn_stats(chain.bst[:, t, :], chain.y[:, t, :]).then_inc(chain.stats, 1)
                    for t in range(QT):
                        dve.wait_ge(chain.stats, chain.n_stats.at(u, t + 1))
                        alone(dve)
                        nc.vector.bn_aggr(chain.bag[:, t, :], chain.bst[:, t, :]).then_inc(chain.stats, 1)
                else:
                    for t in range(QT):
                        if t:
                            dve.wait_ge(chain.stats, chain.n_stats.at(u, t))
                        nc.vector.tensor_tensor_reduce(chain.sq[:, :], chain.y[:, t, :], chain.y[:, t, :], 1.0, 0.0,
                                                       ALU.mult, ALU.add, chain.ysum[:, t:t + 1]
                                                       ).then_inc(chain.stats, 1)

            def apply_norm(chain, u, square):
                dve.wait_ge(chain.root, chain.two.whole(u))
                wait(dve, chain.scaled, chain.one.at(u, 0))
                for t in range(QT):
                    if square:
                        ins = nc.vector.tensor_scalar(chain.z[:, t, :], chain.y[:, t, :], chain.rs[:, t:t + 1], None,
                                                      ALU.mult)
                    else:
                        ins = nc.vector.tensor_scalar(chain.z[:, t, :], chain.y[:, t, :], chain.bag[:, t, 0:1],
                                                      chain.rs[:, t:t + 1], ALU.subtract, ALU.mult)
                    ins.then_inc(chain.normed, 1)

            def take(name, u):
                if name == "XT":
                    dve.wait_ge(ready["XT"], ONE.whole(u))
                    nc.vector.tensor_copy(xT[u.parity][:, PAD:PAD + LQ], misc[:, 0:LQ]).then_inc(taken["XT"], 1)
                elif name == "X2":
                    dve.wait_ge(ready["X2"], FFN.whole(u))
                    nc.vector.tensor_copy(x2T[:, :], misc[:, 0:LQ]).then_inc(taken["X2"], 1)
                elif name == "D":
                    dve.wait_ge(ready["D"], ONE.whole(u))
                    both = misc[:, 0:4 * 72].rearrange("p (g c) -> p g c", g=4)
                    nc.vector.tensor_scalar(den[:, :, :], both[:, :, 64:72], TINY, None, ALU.max
                                            ).then_inc(den_steps, 1)
                    dve.wait_ge(den_steps, TWO.at(u, 1))
                    nc.vector.reciprocal(rden[:, :, :], den[:, :, :]).then_inc(den_steps, 1)
                    dve.wait_ge(den_steps, TWO.at(u, 2))
                    wait(dve, ready["A"], ONE.at(u, 0))
                    nc.vector.tensor_tensor(
                        att[:, :, :].rearrange("p t (r h d) -> p (t r) h d", r=2, d=DH),
                        both[:, :, 0:64].rearrange("p g (h d) -> p g h d", d=DH),
                        rden[:, :, :].rearrange("p g (h o) -> p g h o", o=1).to_broadcast([P, 4, 8, DH]),
                        ALU.mult).then_inc(taken["D"], 1)
                elif name == "O":
                    statistics(attn_norm, u, "O", xb, (xb_ready, ONE.whole(u)), u.stage == 2)
                elif name in ("M0", "M1"):
                    half = int(name[1])
                    dve.wait_ge(ready[name], ONE.whole(u))
                    wait(dve, mrows_loaded[half], DMA1.at(u, 0))
                    nc.vector.tensor_copy(mT[half][:, :], misc_bf[0:3 * H // 2, 0:LQ]).then_inc(taken[name], 1)
                elif name == "F":
                    statistics(ffn_norm, u, "F", x2b, (x2_steps, FFN2.whole(u)), False)
                    apply_norm(ffn_norm, u, False)

            def step(u):
                main, before, nxt, n = in_flight(u)
                unit_of = units(u, before, nxt, n)
                for slot in slots_of(u):
                    if slot.split is not None and unit_of[f"M{slot.split}"] is not None:
                        split_maxima(unit_of[f"M{slot.split}"], slot.split)
                    if slot.raw and before is not None:
                        take_raw(before)
                    for k in (slot.maxima(nxt) if nxt is not None else ()):
                        maximum(nxt, k)
                    for name in slot.small:
                        if has(name, unit_of[name]):
                            take(name, unit_of[name])
                    if slot.norm and before is not None:
                        apply_norm(attn_norm, before, before.stage == 2)

            schedule(dve, step)

        @block.gpsimd
        def _(pool):
            for i in range(2):
                nc.gpsimd.memset(vp[i][:, :, :, :], 0.0).then_inc(pool_set, 1)
                nc.gpsimd.memset(qst[i][0:ROWS_MAX, :, :].bitcast(mybir.dt.uint32), 0).then_inc(pool_set, 1)
                nc.gpsimd.memset(msplit[i][:, :, :], 0.0).then_inc(pool_set, 1)
            pool.wait_ge(x_loaded, 16)
            pool.wait_ge(pool_set, POOL_SETS)
            pool.wait_ge(dve_set, 4)

            def rows_of(t):
                return t.rearrange("p (o d) -> p o d", o=1).to_broadcast([P, QT, D])

            def copy_input(u):
                if u.stage > 0:
                    pool.wait_ge(x_ready, PerUnit(1, 1, 0).whole(Unit(u.stage - 1, u.batch, 0)))
                wait(pool, ready["XT"], ONE.at(u, 0))
                alone(pool)
                nc.gpsimd.tensor_copy(xin[:, :, :], xs[:, u.batch, :, :]).then_inc(x_copied, 1)

            def norm_inputs(u):
                means = PerUnit(0, 0, 2)
                pool.wait_ge(squares_summed, SQUARES.whole(u))
                alone(pool)
                nc.gpsimd.tensor_scalar(nms[:, :], nsum[:, :], 1.0 / D, RMS_EPS, ALU.mult, ALU.add
                                        ).then_inc(means_made, 1)
                pool.wait_ge(means_made, means.at(u, 1))
                nc.gpsimd.tensor_tensor(nrs[:, :], nms[:, :], minushalf[:, 0:QT + CT_N], ALU.pow
                                        ).then_inc(means_made, 1)
                pool.wait_ge(means_made, means.at(u, 2))
                wait(pool, ready["CT"], COUNT["CT"].at(u, 0))
                r = nrs[:, :].rearrange("p (t o) -> p t o", o=1).to_broadcast([P, QT + CT_N, D])
                nc.gpsimd.tensor_tensor(xn[:, :, :], xin[:, :, :], r[:, 0:QT, :], ALU.mult)
                nc.gpsimd.tensor_tensor(cn[:, :, :], cin[u.parity][:, :, :], r[:, QT:, :], ALU.mult
                                        ).then_inc(inputs_normed, 1)

            def split(u, src, rest, parts, n, have, steps):
                pool.wait_ge(have, ONE.whole(u))
                nc.gpsimd.tensor_tensor(rest[:, 0:n], src[:, 0:n], parts[:, 0, 0:n], ALU.subtract).then_inc(steps, 1)
                nc.gpsimd.tensor_tensor(parts[:, 1, 0:n], src[:, 0:n], parts[:, 0, 0:n], ALU.subtract
                                        ).then_inc(steps, 1)
                pool.wait_ge(steps, THREE.at(u, 2))
                nc.gpsimd.tensor_tensor(parts[:, 2, 0:n], rest[:, 0:n], parts[:, 1, 0:n], ALU.subtract
                                        ).then_inc(steps, 1)

            def residual(u):
                wait(pool, taken["O"], ONE.at(u, 0))
                alone(pool)
                if u.stage < 2:
                    pool.wait_ge(bias_made, 4)
                    ins = nc.gpsimd.tensor_tensor(xb[:, :, :], xs[:, u.batch, :, :], rows_of(bo2[u.stage][:, :]),
                                                  ALU.add)
                else:
                    ins = nc.gpsimd.tensor_copy(xb[:, :, :], xs[:, u.batch, :, :])
                ins.then_inc(xb_ready, 1)

            def root(chain, u, square):
                pool.wait_ge(chain.stats, chain.n_stats.whole(u))
                alone(pool)
                if square:
                    nc.gpsimd.tensor_scalar(chain.ms[:, :], chain.ysum[:, :], 1.0 / D, RMS_EPS, ALU.mult, ALU.add
                                            ).then_inc(chain.root, 1)
                else:
                    src = chain.bag[:, :, 1:2].rearrange("p t o -> p (t o)")
                    nc.gpsimd.tensor_scalar(chain.ms[:, :], src, LN_EPS, None, ALU.add).then_inc(chain.root, 1)
                pool.wait_ge(chain.root, chain.two.at(u, 1))
                nc.gpsimd.tensor_tensor(chain.rs[:, :], chain.ms[:, :], minushalf[:, 0:QT], ALU.pow
                                        ).then_inc(chain.root, 1)

            def scale(chain, u, g):
                pool.wait_ge(chain.normed, chain.two.whole(u))
                nc.gpsimd.tensor_tensor(chain.zg[:, :, :], chain.z[:, :, :], rows_of(gam[g]), ALU.mult
                                        ).then_inc(chain.scaled, 1)

            def finish_attention(u):
                root(attn_norm, u, u.stage == 2)
                if u.stage == 2:
                    if not isinstance(u.batch, int) or u.batch > 0:
                        pool.wait_ge(out_stored, u.batch * 16)
                    scale(attn_norm, u, 3)
                    return
                scale(attn_norm, u, u.stage)
                pool.wait_ge(attn_norm.scaled, ONE.whole(u))
                if u.stage == 0:
                    alone(pool)
                    nc.gpsimd.tensor_tensor(xs[:, u.batch, :, :], attn_norm.zg[:, :, :], rows_of(bet[0]), ALU.add
                                            ).then_inc(x_ready, 1)
                else:
                    wait(pool, ready["X2"], FFN.at(u, 0)) if isinstance(u.batch, int) else None
                    nc.gpsimd.tensor_tensor(x2[:, :, :], attn_norm.zg[:, :, :], rows_of(bet[1]), ALU.add
                                            ).then_inc(x2_steps, 1)
                    pool.wait_ge(x2_steps, FFN2.at(u, 1))
                    nc.gpsimd.tensor_tensor(x2b[:, :, :], x2[:, :, :], rows_of(b2b), ALU.add).then_inc(x2_steps, 1)

            def finish_feed_forward(u):
                root(ffn_norm, u, False)
                scale(ffn_norm, u, 2)
                pool.wait_ge(ffn_norm.scaled, FFN.whole(u))
                alone(pool)
                nc.gpsimd.tensor_tensor(xs[:, u.batch, :, :], ffn_norm.zg[:, :, :], rows_of(bet[2]), ALU.add
                                        ).then_inc(x_ready, 1)

            def step(u):
                main, before, nxt, n = in_flight(u)
                if n is not None:
                    copy_input(n)
                    if n.stage == 2:
                        norm_inputs(n)
                if before is not None:
                    residual(before)
                if n is not None:
                    split(n, qf, qr, qs, LQ, taken["Q"], q_steps)
                    split(n, kf, kr, ks, KEYS[n.stage], taken["K"], k_steps)
                if before is not None:
                    finish_attention(before)
                    if before.stage == 1:
                        finish_feed_forward(before)

            schedule(pool, step)



def shape_constants():
    bf = np.dtype("bfloat16")
    c = {}
    c["c_ident"] = np.eye(P, dtype=np.float32)
    c["c_identb"] = np.eye(P, dtype=np.float32).astype(bf)
    j = np.arange(2 * BLK)[:, None]
    i = np.arange(BLK)[None, :]
    band = (j <= i + BLK) & (j > i)
    first = band & (j >= BLK)
    c["c_mask_t"] = np.where(np.concatenate([first] + [band] * (NBLK - 1), 1), 0.0, NEG).astype(bf)
    c["c_mask_q"] = np.where(np.stack([np.concatenate([first.T, band.T]), np.concatenate([band.T, band.T])], 1),
                             0.0, NEG).astype(bf)
    pick = np.zeros((P, 72), np.float32)
    for gg in range(2):
        for j4 in range(4):
            for d in range(DH):
                pick[32 * j4 + 16 * gg + d, DH * (4 * gg + j4) + d] = 1.0
            pick[32 * j4 + 16 * gg + DH, 64 + 4 * gg + j4] = 1.0
    c["c_pick"] = pick
    slope = 2.0 ** (-8.0 * np.arange(1, H + 1) / H)
    place = np.arange(PAD + LQ) - (PAD + LQ) // 2
    rest = (slope[:, None] * place[None, :] / SCALE)
    parts = []
    for _ in range(3):
        parts.append(rest.astype(bf))
        rest = rest - parts[-1].astype(np.float64)
    c["c_slopes"] = np.stack(parts)
    c["c_ones"] = np.ones((3, H, LQ), bf)
    c["c_zeros"] = np.zeros((3, H // 2, LK), bf)
    return c


def kernel(**inputs):
    import concourse.bacc as _bacc
    from concourse import mybir as _mybir
    from concourse.bass_utils import run_bass_kernel_spmd as _run

    nc = _bacc.Bacc("TRN2", target_bir_lowering=False, num_devices=1)
    given = dict(inputs)

    def take(*names):
        return [np.asarray(given.pop(n)) for n in names]

    given["w_in"] = np.stack(take("L0_xattn_swq", "L0_xattn_swk", "L0_xattn_swv", "L0_xattn_cwq", "L0_xattn_cwk",
                                  "L0_xattn_cwv", "L1_xattn_Wq", "L1_xattn_Wk", "L1_xattn_Wv"), 1)
    given["w_out"] = np.stack(take("L0_xattn_swo", "L0_xattn_cwo", "L1_xattn_Wo"), 1)
    given["columns"] = np.concatenate(
        [v.reshape(-1, P).T for v in take("L0_xattn_sbq", "L0_xattn_sbk", "L0_xattn_cbq", "L0_xattn_cbk",
                                          "L1_xattn_g_q", "L1_xattn_g_c", "L0_xattn_b1",
                                          "L0_xattn_sbv", "L0_xattn_cbv")], 1)
    given["vectors"] = np.stack(take("L0_xattn_sbo", "L0_xattn_cbo", "L0_xattn_b2", "L0_xattn_g1", "L0_xattn_g2",
                                     "L0_xattn_g3", "L1_xattn_g_out", "L0_xattn_be1", "L0_xattn_be2",
                                     "L0_xattn_be3"))
    given.update(shape_constants())
    arrays, args = {}, {}
    for name, value in given.items():
        value = np.ascontiguousarray(value)
        arrays[f"in_{name}_dram"] = value
        args[name] = nc.dram_tensor(f"in_{name}_dram", value.shape, _mybir.dt.from_np(value.dtype),
                                    kind="ExternalInput").ap()
    out = nc.dram_tensor("out_0_dram", (B, LQ, D), F32, kind="ExternalOutput").ap()
    two_layer_kernel(nc, args, out)
    r = _run(nc, [arrays], core_ids=[0])
    return r.results[0]["out_0_dram"]
```
